# Optimizing a Trainium2 kernel written in Bass

```python
import numpy as np
import jax
import jax.numpy as jnp

def _softmax(x, axis=-1):
    return jax.nn.softmax(x, axis=axis)

def _gelu(x):
    return jax.nn.gelu(x, approximate=True)

def _silu(x):
    return jax.nn.silu(x)

def _sigmoid(x):
    return jax.nn.sigmoid(x)

def _layernorm(x, axis=-1, eps=1e-05):
    m = jnp.mean(x, axis=axis, keepdims=True)
    v = jnp.var(x, axis=axis, keepdims=True)
    return (x - m) / jnp.sqrt(v + eps)

def _scatter_add(tgt, idx, src, axis=0):
    return tgt.at[idx].add(src)

def _segment_sum(src, seg, n):
    return jax.ops.segment_sum(src, seg, n)
kernel_name = 'mk_metaformer_d1_conv_nchw384_r4_fc019b'

def setup_inputs(seed: int=0):
    np.random.seed(seed)
    _w = jnp.asarray

    def _rec_inputs():
        import jax
        import jax.numpy as jnp
        _gk = jax.random.key(seed)
        x = -0.0003483 + 1 * jax.random.normal(jax.random.fold_in(_gk, 1), (1, 96, 48, 48), jnp.float32)
        return x
    x = _rec_inputs()

    def _L0_conv_setup():
        import jax, jax.numpy as jnp
        import numpy as np
        from jax import lax
        DIM = 96
        HEADS = 8
        DS = 2

        def _topk_softmax(attn, kk):
            idx = lax.top_k(attn, kk)[1]
            mask = jax.nn.one_hot(idx, attn.shape[-1], dtype=attn.dtype).sum(-2)
            return jax.nn.softmax(jnp.where(mask > 0, attn, -jnp.inf), axis=-1)
        key = jax.random.key(seed)
        ks = jax.random.split(key, 6)
        d = DIM
        x = jax.random.normal(ks[0], (1, d, 48, 48), jnp.float32)
        w_qkv = jax.random.normal(ks[1], (3 * d, d), jnp.float32) * 0.02
        b_qkv = jnp.zeros((3 * d,), jnp.float32)
        w_dw = jax.random.normal(ks[2], (3 * d, 1, 3, 3), jnp.float32) * 0.1
        b_dw = jnp.zeros((3 * d,), jnp.float32)
        w_proj = jax.random.normal(ks[3], (d, d), jnp.float32) * 0.02
        b_proj = jnp.zeros((d,), jnp.float32)
        temperature = jnp.ones((HEADS, 1, 1), jnp.float32)
        a1 = jnp.array([0.2], jnp.float32)
        a2 = jnp.array([0.2], jnp.float32)
        a3 = jnp.array([0.2], jnp.float32)
        a4 = jnp.array([0.2], jnp.float32)
        return {'x': x, 'w_qkv': w_qkv, 'b_qkv': b_qkv, 'w_dw': w_dw, 'b_dw': b_dw, 'w_proj': w_proj, 'b_proj': b_proj, 'temperature': temperature, 'a1': a1, 'a2': a2, 'a3': a3, 'a4': a4}
    _L0_conv_all = _L0_conv_setup()
    _L0_conv_in = {k: v for k, v in _L0_conv_all.items() if k in ('w_qkv', 'b_qkv', 'w_dw', 'b_dw', 'w_proj', 'b_proj', 'temperature', 'a1', 'a2', 'a3', 'a4')}
    del _L0_conv_all

    def _L0_ffn_setup():
        import jax, jax.numpy as jnp
        import numpy as np
        NUM_EXPERTS = 4
        TOP_K = 2
        DIM = 96
        HID = 4 * DIM
        key = jax.random.key(seed)
        ks = jax.random.split(key, 5)
        B, S = (16, 512)
        scale_in = 1.0 / np.sqrt(DIM)
        scale_hid = 1.0 / np.sqrt(HID)
        return {'x': jax.random.normal(ks[0], (B, S, DIM), dtype=jnp.float32), 'gate_w': jax.random.normal(ks[1], (DIM, NUM_EXPERTS), dtype=jnp.float32) * scale_in, 'gate_b': jnp.zeros((NUM_EXPERTS,), dtype=jnp.float32), 'w1': jax.random.normal(ks[2], (NUM_EXPERTS, DIM, HID), dtype=jnp.float32) * scale_in, 'b1': jnp.zeros((NUM_EXPERTS, HID), dtype=jnp.float32), 'w2': jax.random.normal(ks[3], (NUM_EXPERTS, HID, DIM), dtype=jnp.float32) * scale_hid, 'b2': jnp.zeros((NUM_EXPERTS, DIM), dtype=jnp.float32)}
    _L0_ffn_all = _L0_ffn_setup()
    _L0_ffn_in = {k: v for k, v in _L0_ffn_all.items() if k in ('gate_w', 'gate_b', 'w1', 'b1', 'w2', 'b2')}
    del _L0_ffn_all
    return {'x': x, 'L0_conv_w_qkv': _L0_conv_in['w_qkv'], 'L0_conv_b_qkv': _L0_conv_in['b_qkv'], 'L0_conv_w_dw': _L0_conv_in['w_dw'], 'L0_conv_b_dw': _L0_conv_in['b_dw'], 'L0_conv_w_proj': _L0_conv_in['w_proj'], 'L0_conv_b_proj': _L0_conv_in['b_proj'], 'L0_conv_temperature': _L0_conv_in['temperature'], 'L0_conv_a1': _L0_conv_in['a1'], 'L0_conv_a2': _L0_conv_in['a2'], 'L0_conv_a3': _L0_conv_in['a3'], 'L0_conv_a4': _L0_conv_in['a4'], 'L0_ffn_gate_w': _L0_ffn_in['gate_w'], 'L0_ffn_gate_b': _L0_ffn_in['gate_b'], 'L0_ffn_w1': _L0_ffn_in['w1'], 'L0_ffn_b1': _L0_ffn_in['b1'], 'L0_ffn_w2': _L0_ffn_in['w2'], 'L0_ffn_b2': _L0_ffn_in['b2']}

def reference(x, L0_conv_w_qkv, L0_conv_b_qkv, L0_conv_w_dw, L0_conv_b_dw, L0_conv_w_proj, L0_conv_b_proj, L0_conv_temperature, L0_conv_a1, L0_conv_a2, L0_conv_a3, L0_conv_a4, L0_ffn_gate_w, L0_ffn_gate_b, L0_ffn_w1, L0_ffn_b1, L0_ffn_w2, L0_ffn_b2):
    import jax
    import jax.numpy as jnp

    def _L0_conv_ref(x, w_qkv, b_qkv, w_dw, b_dw, w_proj, b_proj, temperature, a1, a2, a3, a4):
        import jax, jax.numpy as jnp
        import numpy as np
        from jax import lax
        DIM = 96
        HEADS = 8
        DS = 2

        def _topk_softmax(attn, kk):
            idx = lax.top_k(attn, kk)[1]
            mask = jax.nn.one_hot(idx, attn.shape[-1], dtype=attn.dtype).sum(-2)
            return jax.nn.softmax(jnp.where(mask > 0, attn, -jnp.inf), axis=-1)
        b, c, h, w = x.shape
        qkv = jnp.einsum('bchw,oc->bohw', x, w_qkv) + b_qkv[None, :, None, None]
        hs, ws = (h // DS, w // DS)
        qkv = qkv.reshape(b, 3 * c, hs, DS, ws, DS).max(axis=(3, 5))
        qkv = lax.conv_general_dilated(qkv, w_dw, (1, 1), 'SAME', feature_group_count=3 * c, dimension_numbers=('NCHW', 'OIHW', 'NCHW'))
        qkv = qkv + b_dw[None, :, None, None]
        q, k, v = jnp.split(qkv, 3, axis=1)
        hw = hs * ws
        C = c // HEADS
        q = q.reshape(b, HEADS, C, hw)
        k = k.reshape(b, HEADS, C, hw)
        v = v.reshape(b, HEADS, C, hw)
        q = q / jnp.clip(jnp.linalg.norm(q, axis=-1, keepdims=True), 1e-12)
        k = k / jnp.clip(jnp.linalg.norm(k, axis=-1, keepdims=True), 1e-12)
        attn = jnp.einsum('bhcn,bhdn->bhcd', q, k) * temperature[None]
        out = _topk_softmax(attn, C // 2) @ v * a1 + _topk_softmax(attn, C * 2 // 3) @ v * a2 + _topk_softmax(attn, C * 3 // 4) @ v * a3 + _topk_softmax(attn, C * 4 // 5) @ v * a4
        out = out.reshape(b, c, hs, ws)
        out = jax.nn.gelu(out, approximate=False)
        out = jnp.repeat(jnp.repeat(out, DS, axis=2), DS, axis=3)
        out = jnp.einsum('bchw,oc->bohw', out, w_proj) + b_proj[None, :, None, None]
        return out

    def _L0_ffn_ref(x, gate_w, gate_b, w1, b1, w2, b2):
        import jax, jax.numpy as jnp
        import numpy as np
        NUM_EXPERTS = 4
        TOP_K = 2
        DIM = 96
        HID = 4 * DIM
        scores = jnp.einsum('bsd,de->bse', x, gate_w) + gate_b
        probs = jax.nn.softmax(scores, axis=-1)
        topk_vals, topk_idx = jax.lax.top_k(probs, TOP_K)
        mask = jnp.sum(jax.nn.one_hot(topk_idx, NUM_EXPERTS, dtype=probs.dtype), axis=-2)
        masked = probs * mask
        masked = masked / (jnp.sum(masked, axis=-1, keepdims=True) + 1e-09)
        h = jax.nn.gelu(jnp.einsum('bsd,edh->ebsh', x, w1) + b1[:, None, None, :], approximate=False)
        y = jnp.einsum('ebsh,ehd->ebsd', h, w2) + b2[:, None, None, :]
        out = jnp.einsum('bse,ebsd->bsd', masked, y)
        return out

    def _gn(v, G=32, eps=1e-05):
        B_, C_, H_, W_ = v.shape
        g = v.reshape(B_, G, C_ // G, H_, W_)
        m = jnp.mean(g, axis=(2, 3, 4), keepdims=True)
        s = jnp.var(g, axis=(2, 3, 4), keepdims=True)
        return ((g - m) / jnp.sqrt(s + eps)).reshape(v.shape)

    def _ln_c(v, eps=1e-06):
        m = jnp.mean(v, axis=1, keepdims=True)
        s = jnp.var(v, axis=1, keepdims=True)
        return (v - m) / jnp.sqrt(s + eps)

    def _ln_t(v, eps=1e-05):
        m = jnp.mean(v, axis=-1, keepdims=True)
        s = jnp.var(v, axis=-1, keepdims=True)
        return (v - m) / jnp.sqrt(s + eps)

    def _to_tokens(v):
        B_, C_, H_, W_ = v.shape
        return v.reshape(B_, C_, H_ * W_).transpose(0, 2, 1)

    def _from_tokens(t, like):
        B_, C_, H_, W_ = like.shape
        return t.transpose(0, 2, 1).reshape(B_, C_, H_, W_)
    x = x + _L0_conv_ref(_ln_c(x), L0_conv_w_qkv, L0_conv_b_qkv, L0_conv_w_dw, L0_conv_b_dw, L0_conv_w_proj, L0_conv_b_proj, L0_conv_temperature, L0_conv_a1, L0_conv_a2, L0_conv_a3, L0_conv_a4)
    t = _to_tokens(x)
    t = t + _L0_ffn_ref(_ln_t(t), L0_ffn_gate_w, L0_ffn_gate_b, L0_ffn_w1, L0_ffn_b1, L0_ffn_w2, L0_ffn_b2)
    x = _from_tokens(t, x)
    return x

_drawn_inputs = setup_inputs


def setup_inputs(seed=0):
    import zlib

    import numpy as np

    out = dict(_drawn_inputs(seed))
    spreads = {'L0_conv_b_qkv': (0.0, 0.8),
     'L0_conv_b_dw': (0.0, 0.8),
     'L0_conv_b_proj': (0.0, 0.1),
     'L0_conv_temperature': (1.0, 0.6),
     'L0_ffn_gate_b': (0.0, 0.1),
     'L0_ffn_b1': (0.0, 0.1),
     'L0_ffn_b2': (0.0, 0.1)}
    factors = {'L0_conv_w_qkv': 8.0, 'L0_conv_w_dw': 8.0, 'L0_conv_w_proj': 5.446}
    for name, (base, spread) in spreads.items():
        noise = np.random.default_rng([zlib.crc32(name.encode()), seed]).standard_normal(out[name].shape)
        drawn = base * np.exp(spread * noise) if base else spread * noise
        out[name] = jnp.asarray(drawn.astype(out[name].dtype))
    for name, factor in factors.items():
        out[name] = (out[name] * factor).astype(out[name].dtype)
    return out
```

```python
import concourse.bass as bass
from concourse import mybir
from contextlib import ExitStack

F32 = mybir.dt.float32
F32R = mybir.dt.float32r
BF16 = mybir.dt.bfloat16
I32 = mybir.dt.int32
ALU = mybir.AluOpType
ACT = mybir.ActivationFunctionType
AX = mybir.AxisListType

C = 96
IMG = 48
TOK = IMG * IMG
POOL = IMG // 2
PIX = POOL * POOL
PAD = POOL + 2
HEADS = 8
DH = C // HEADS
KEEP = (DH // 2, DH * 2 // 3, DH * 3 // 4, DH * 4 // 5)
E = 4
HID = 4 * C
HT = HID // 128
NH = E * HT
CH = 384
NCH = TOK // CH
TPC = CH // 128
NT = TOK // 128
HALF = NCH // 2
NPAIR = NH // 2
LAG = 2
HB = 3
BANK = 512
TB = PIX // C
HP = PIX // 2

P_QKV = 0
P_PROJ = P_QKV + 3 * C
P_GATE = P_PROJ + C
P_DW = P_GATE + E
P_BDW = P_DW + 27
P_BPROJ = P_BDW + 3
P_TEMP = P_BPROJ + 1
P_A = P_TEMP + 1
P_B2 = P_A + 4
P_END = P_B2 + E

K_ID = 0
K_CEN = K_ID + 128
K_BLK = K_CEN + C
K_TRI = K_BLK + C
K_TRIE = K_TRI + DH * DH
K_SEL = K_TRIE + E * E
K_END = K_SEL + E * C


def last_pair(e):
    return (HT * e + HT - 1) // 2


def build(nc, x, par, b1, w1, w2, const, out):
    ctx = ExitStack()
    with ctx:
        def sb(name, shape, dt=F32):
            return ctx.enter_context(nc.sbuf_tensor(name, shape, dt))

        def sem(name):
            return ctx.enter_context(nc.semaphore(name))

        psum = ctx.enter_context(nc.psum_tensor("psum", [128, 8 * BANK], F32))

        def bank(b, rows=C, cols=BANK, at=0):
            return psum[0:rows, b * BANK + at:b * BANK + at + cols]

        xs = sb("xs", [C, TOK])
        pars = sb("pars", [C + 1, P_END])
        cst = sb("cst", [128, K_END])
        ident = cst[:, K_ID:K_ID + 128]
        ident_r = sb("ident_r", [128, 128], F32R)
        ident_b = sb("ident_b", [128, 128], BF16)
        sel_b = sb("sel_b", [128, E * C], BF16)
        mean_w = sb("mean_w", [C, 1])
        w1s = sb("w1s", [C + 1, E * HID])
        w1_hi = sb("w1_hi", [C + 1, E * HID], F32R)
        w1_lo = sb("w1_lo", [C + 1, E * HID], F32R)
        w2s = sb("w2s", [128, NH * C])
        w2_hi = sb("w2_hi", [128, NH * C], F32R)
        w2_lo = sb("w2_lo", [128, NH * C], F32R)
        xc = sb("xc", [C, TOK])
        sq = sb("sq", [C, TOK])
        xn = sb("xn", [C + 1, TOK])
        xn_hi = sb("xn_hi", [C + 1, TOK], F32R)
        xn_lo = sb("xn_lo", [C + 1, TOK], F32R)
        var = sb("var", [128, NT])
        seed = sb("seed", [128, NT])
        nhalf = sb("nhalf", [128, NT])
        newton = sb("newton", [128, NT])
        rs_hi = sb("rs_hi", [128, NT], F32R)
        rs_lo = sb("rs_lo", [128, NT], F32R)
        pooled = sb("pooled", [C, 3 * PAD * PAD])
        qkc = sb("qkc", [C, 2 * PIX])
        qkT = sb("qkT", [C, 2 * PIX])
        vc = sb("vc", [C, PIX])
        diag = sb("diag", [C, 9 * C])
        sqj = sb("sqj", [C, PIX])
        ssq = sb("ssq", [C, 2])
        n2 = sb("n2", [C, 2])
        n2h = sb("n2h", [C, 2])
        n2t = sb("n2t", [C, 2])
        rnorm = sb("rnorm", [C, 2])
        rqt = sb("rqt", [C, 1])
        rk_blk = sb("rk_blk", [C, C])
        sc_blk = sb("sc_blk", [C, C])
        sc = sb("sc", [C, DH])
        nmax = sb("nmax", [C, 1])
        ex = sb("ex", [C, DH])
        above = sb("above", [C, DH * DH])
        equal = sb("equal", [C, DH * DH])
        rank = sb("rank", [C, DH])
        kept = sb("kept", [C, 4 * DH])
        ksum = sb("ksum", [C, 4])
        coef = sb("coef", [C, 4])
        att = sb("att", [C, DH])
        att_blk = sb("att_blk", [C, C])
        attT = sb("attT", [C, C])
        go = sb("go", [C, PIX])
        pr = sb("pr", [C, PIX])
        gs = sb("gs", [128, NT * E])
        gm = sb("gm", [128, NT])
        ge = sb("ge", [128, NT * E])
        gcmp = sb("gcmp", [128, NT * E * E])
        geq = sb("geq", [128, NT * E * E])
        grank = sb("grank", [128, NT * E])
        gate = sb("gate", [128, NT * E])
        gparts = sb("gparts", [128, NT * 3 * E], BF16)
        gateT = sb("gateT", [128, TOK], BF16)
        gb = sb("gb", [C, 2 * CH])
        hf = sb("hf", [128, 2 * 2 * CH])
        h_hi = sb("h_hi", [128, HB * 2 * CH], F32R)
        h_lo = sb("h_lo", [128, HB * 2 * CH], F32R)
        yg = sb("yg", [C, 2 * CH])

        x_in = [sem(f"x_in{i}") for i in range(3)]
        par_in, cst_in, w1_in, w2_in = sem("par_in"), sem("cst_in"), sem("w1_in"), sem("w2_in")
        ones_set = sem("ones_set")
        rows_set = sem("rows_set")
        ident_set = sem("ident_set")
        diag_set = sem("diag_set")
        sel_set = sem("sel_set")
        w_split = sem("w_split")
        dve_chain = sem("dve_chain")
        act_chain = sem("act_chain")
        pool_chain = sem("pool_chain")
        ln = [{n: sem(f"ln{i}_{n}") for n in
               ("centred", "xc", "sq", "var", "rstd", "spread", "xn")} for i in range(2)]
        qkv_done, pool_done = sem("qkv_done"), sem("pool_done")
        conv_done = sem("conv_done")
        vconv_done, v_ready = sem("vconv_done"), sem("v_ready")
        ssq_done, rnorm_done = sem("ssq_done"), sem("rnorm_done")
        qkT_done, qkT_copied = sem("qkT_done"), sem("qkT_copied")
        rk_spread, score_done = sem("rk_spread"), sem("score_done")
        nmax_done, exp_done = sem("nmax_done"), sem("exp_done")
        att_ready, attT_done, attT_copied = sem("att_ready"), sem("attT_done"), sem("attT_copied")
        av_done, gelu_o, proj_done, proj_ready = sem("av_done"), sem("gelu_o"), sem("proj_done"), sem("proj_ready")
        x2_ready = sem("x2_ready")
        split_hi, split_lo = sem("split_hi"), sem("split_lo")
        gscore_done, gsub_done, gexp_done, gparts_done = (
            sem("gscore_done"), sem("gsub_done"), sem("gexp_done"), sem("gparts_done"))
        gT_done, gT_copied = sem("gT_done"), sem("gT_copied")
        l1_done, gelu_done, h_split, l2_done = sem("l1_done"), sem("gelu_done"), sem("h_split"), sem("l2_done")
        gb_done, gb_copied, y_gated, acc_done = sem("gb_done"), sem("gb_copied"), sem("y_gated"), sem("acc_done")
        out_done = sem("out_done")

        block = ctx.enter_context(nc.Block())

        def padded(g):
            return pooled[:, g * PAD * PAD:(g + 1) * PAD * PAD].rearrange("p (a b) -> p a b", b=PAD)

        def tap(g, t, r0=0, rows=POOL):
            dy, dx = divmod(t, 3)
            return padded(g)[:, r0 + dy:r0 + dy + rows, dx:dx + POOL]

        def grid(ap):
            return ap.rearrange("p (a b) -> p a b", b=POOL)

        def cols(ap, c, n=CH):
            return ap[:, bass.ds(c * n, n)]

        @block.sync
        def _(sp):
            third = TOK // 3
            sp.dma_start(xs[:, 0:third], x[:, 0:third]).then_inc(x_in[0], 16)
            sp.dma_start(pars[:, :], par).then_inc(par_in, 16)
            sp.dma_start(xs[:, 2 * third:], x[:, 2 * third:]).then_inc(x_in[2], 16)
            sp.dma_start(w2s[:, :].rearrange("p (j d) -> p j d", d=C),
                         w2.rearrange("e (t p) d -> p (e t) d", p=128)).then_inc(w2_in, 16)
            with sp.Fori(0, NCH) as c:
                sp.wait_ge(acc_done, c * E + E)
                sp.dma_start(out[:, bass.ds(c * CH, CH)], cols(xs, c)).then_inc(out_done, 16)
            sp.wait_ge(out_done, 16 * NCH)

        @block.gpsimd
        def _(pool):
            chain = [0]

            def link(ins):
                chain[0] += 1
                ins.then_inc(pool_chain, 1)
                pool.wait_ge(pool_chain, chain[0])

            pool.memset(mean_w[:, :], 1.0 / C).then_inc(ones_set, 1)
            pool.memset(pooled[:, :], 0.0).then_inc(ones_set, 1)
            pool.memset(gateT[:, :].bitcast(F32), 0.0).then_inc(ones_set, 1)
            pool.wait_ge(par_in, 16)
            pool.wait_ge(cst_in, 16)
            for t in range(9):
                pool.tensor_scalar(diag[:, t * C:(t + 1) * C], ident[0:C, 0:C],
                                   pars[0:C, P_DW + 18 + t:P_DW + 19 + t], None, ALU.mult).then_inc(diag_set, 1)
            pool.tensor_copy(sel_b[:, :], cst[:, K_SEL:K_SEL + E * C]).then_inc(sel_set, 1)
            pool.wait_ge(w_split, 2)
            pool.tensor_tensor(w1_lo[:, :], w1s[:, :], w1_hi[:, :].bitcast(F32), ALU.subtract).then_inc(w_split, 1)
            pool.tensor_tensor(w2_lo[:, :], w2s[:, :], w2_hi[:, :].bitcast(F32), ALU.subtract).then_inc(w_split, 1)
            for c in range(NCH):
                pool.wait_ge(split_hi, c + 1)
                pool.tensor_tensor(cols(xn_lo, c)[0:C], cols(xn, c)[0:C], cols(xn_hi, c)[0:C].bitcast(F32),
                                   ALU.subtract).then_inc(split_lo, 1)
            for c in range(NCH):
                for e in range(E):
                    pool.wait_ge(y_gated, c * E + e + 1)
                    if e:
                        pool.wait_ge(acc_done, c * E + e)
                    pool.tensor_tensor(cols(xs, c), cols(xs, c), cols(yg, e % 2), ALU.add).then_inc(acc_done, 1)

        def ln_scalar(act, i, ready):
            s = ln[i]
            for c in range(NCH):
                act.wait_ge(s["centred"], c + 1)
                act.activation(cols(xc, c), bank(ready[c % 2], cols=CH), ACT.Copy).then_inc(s["xc"], 1)
                act.activation(cols(sq, c), bank(ready[c % 2], cols=CH), ACT.Square).then_inc(s["sq"], 1)

        @block.scalar
        def _(act):
            third = TOK // 3
            act.dma_start(cst[:, :], const).then_inc(cst_in, 16)
            act.dma_start(xs[:, third:2 * third], x[:, third:2 * third]).then_inc(x_in[1], 16)
            act.dma_start(w1s[0:C, :].rearrange("p (e h) -> p e h", e=E),
                          w1.rearrange("e d h -> d e h")).then_inc(w1_in, 16)
            act.dma_start(w1s[C:C + 1, :], b1).then_inc(w1_in, 16)
            act.wait_ge(cst_in, 16)
            act.activation(ident_r[:, :], ident, ACT.Copy).then_inc(ident_set, 1)
            act.activation(ident_b[:, :], ident, ACT.Copy).then_inc(ident_set, 1)
            ln_scalar(act, 0, (0, 1))
            act.wait_ge(w1_in, 32)
            act.activation(w1_hi[:, :], w1s[:, :], ACT.Copy).then_inc(w_split, 1)
            act.wait_ge(w2_in, 16)
            act.activation(w2_hi[:, :], w2s[:, :], ACT.Copy).then_inc(w_split, 1)
            for n, g in enumerate((1, 0)):
                act.wait_ge(conv_done, n + 1)
                act.activation(sqj[:, :], qkc[:, g * PIX:(g + 1) * PIX], ACT.Square,
                               accum_out=ssq[:, g:g + 1]).then_inc(ssq_done, 1)
                act.wait_ge(ssq_done, n + 1)
                for b in range(2):
                    act.wait_ge(qkT_done, 2 * n + b + 1)
                    act.activation(qkT[:, g * PIX + b * HP:g * PIX + (b + 1) * HP],
                                   bank(4 + 2 * g + b, cols=HP), ACT.Copy).then_inc(qkT_copied, 1)
            for b in range(2):
                act.wait_ge(vconv_done, b + 1)
                act.activation(vc[:, b * HP:(b + 1) * HP], bank(2 + b, cols=HP), ACT.Identity,
                               bias=pars[0:C, P_BDW + 2:P_BDW + 3]).then_inc(v_ready, 1)
            act.wait_ge(nmax_done, 1)
            act.activation(ex[:, :], sc[:, :], ACT.Exp, bias=nmax[:, 0:1]).then_inc(exp_done, 1)
            for b in range(2):
                act.wait_ge(av_done, b + 1)
                act.activation(go[:, b * HP:(b + 1) * HP], bank(6 + b, cols=HP), ACT.Gelu).then_inc(gelu_o, 1)
            for b in range(2):
                act.wait_ge(proj_done, b + 1)
                act.activation(pr[:, b * HP:(b + 1) * HP], bank(b, cols=HP), ACT.Identity,
                               bias=pars[0:C, P_BPROJ:P_BPROJ + 1]).then_inc(proj_ready, 1)
            ln_scalar(act, 1, (4, 5))
            for c in range(NCH):
                act.wait_ge(ln[1]["xn"], c + 1)
                act.activation(cols(xn_hi, c), cols(xn, c), ACT.Copy).then_inc(split_hi, 1)
            act.wait_ge(gsub_done, 1)
            act.activation(ge[:, :], gs[:, :], ACT.Exp).then_inc(gexp_done, 1)

            def gates(c, q):
                for e in range(E):
                    if last_pair(e) - 1 == q:
                        act.wait_ge(gb_done, c * E + e + 1)
                        if not (isinstance(c, int) and c == 0 and e < 2):
                            act.wait_ge(y_gated, c * E + e - 1)
                        act.activation(cols(gb, e % 2), bank(6 + e % 2, cols=CH), ACT.Copy).then_inc(gb_copied, 1)

            def chunk(c, first=False):
                for p in range(NPAIR):
                    act.wait_ge(l1_done, c * NPAIR + p + 1)
                    if not (first and p < 2):
                        act.wait_ge(h_split, 2 * (c * NPAIR + p - 1))
                    act.activation(cols(hf, p % 2, 2 * CH).rearrange("p (j n) -> p j n", n=CH),
                                   psum[:, (p % 2) * 2 * BANK:(p % 2 + 1) * 2 * BANK]
                                   .rearrange("p (j n) -> p j n", n=BANK)[:, :, 0:CH],
                                   ACT.Gelu).then_inc(gelu_done, 1)
                    if first and p == 0:
                        act.wait_ge(ones_set, 3)
                        for b in range(3):
                            act.wait_ge(gT_done, b + 1)
                            act.activation(gateT[0:3 * E, b * 768:(b + 1) * 768],
                                           psum[0:3 * E, (6 + b % 2) * BANK:(6 + b % 2) * BANK + 384].bitcast(BF16),
                                           ACT.Copy).then_inc(gT_copied, 1)
                    if p >= LAG:
                        gates(c, p - LAG)
                    elif not first:
                        gates(c - 1, p - LAG + NPAIR)

            chunk(0, True)
            with act.Fori(1, NCH) as c:
                chunk(c)
            for q in range(NPAIR - LAG, NPAIR):
                gates(NCH - 1, q)

        @block.vector
        def _(dve):
            chain = [0]

            def link(ins):
                chain[0] += 1
                ins.then_inc(dve_chain, 1)
                dve.wait_ge(dve_chain, chain[0])

            def rsqrt(y, v, nh, t):
                link(dve.tensor_scalar(y.bitcast(I32), v.bitcast(I32), -0.5, 1597463007.0, ALU.mult, ALU.add))
                link(dve.tensor_scalar(nh, v, -0.5, None, ALU.mult))
                for _ in range(3):
                    link(dve.tensor_tensor(t, y, y, ALU.mult))
                    link(dve.tensor_tensor(t, t, nh, ALU.mult))
                    link(dve.scalar_tensor_tensor(y, t, 1.5, y, ALU.add, ALU.mult))

            def ln_vector(i, eps, spread_banks):
                s = ln[i]
                for half in range(2):
                    w = HALF * TPC
                    z = slice(half * w, (half + 1) * w)
                    dve.wait_ge(s["var"], half + 1)
                    link(dve.tensor_scalar(var[:, z], bank(2 + half, 128, w), eps, None, ALU.add))
                    rsqrt(seed[:, z], var[:, z], nhalf[:, z], newton[:, z])
                    link(dve.tensor_copy(rs_hi[:, z], seed[:, z]))
                    dve.tensor_tensor(rs_lo[:, z], seed[:, z], rs_hi[:, z].bitcast(F32),
                                      ALU.subtract).then_inc(s["rstd"], 1)
                    for c in range(half * HALF, (half + 1) * HALF):
                        dve.wait_ge(s["spread"], c + 1)
                        dve.wait_ge(s["xc"], c + 1)
                        dve.tensor_tensor(cols(xn, c)[0:C], bank(spread_banks[c % 2], cols=CH), cols(xc, c),
                                          ALU.mult).then_inc(s["xn"], 1)

            dve.memset(xn[C:C + 1, :], 1.0).then_inc(rows_set, 1)
            dve.memset(xn_lo[C:C + 1, :].bitcast(F32), 0.0).then_inc(rows_set, 1)
            ln_vector(0, 1e-6, (4, 5))
            n = 0
            for g in (1, 0, 2):
                for c in range(NCH):
                    dve.wait_ge(qkv_done, n + 1)
                    src = bank((6, 7, 0, 1)[n % 4], cols=CH).rearrange(
                        "p (a y b x) -> p a b y x", y=2, b=POOL, x=2)
                    dve.tensor_reduce(padded(g)[:, 1 + 4 * c:5 + 4 * c, 1:1 + POOL], src, AX.XY,
                                      ALU.max).then_inc(pool_done, 1)
                    n += 1
            for n, g in enumerate((1, 0)):
                dve.wait_ge(pool_done, 6 * (n + 1))
                o = grid(qkc[:, g * PIX:(g + 1) * PIX])
                link(dve.tensor_scalar(o, tap(g, 0), pars[0:C, P_DW + 9 * g:P_DW + 9 * g + 1],
                                       pars[0:C, P_BDW + g:P_BDW + g + 1], ALU.mult, ALU.add))
                for t in range(1, 9):
                    ins = dve.scalar_tensor_tensor(o, tap(g, t), pars[0:C, P_DW + 9 * g + t:P_DW + 9 * g + t + 1],
                                                   o, ALU.mult, ALU.add)
                    if t < 8:
                        link(ins)
                    else:
                        ins.then_inc(conv_done, 1)
            dve.wait_ge(ssq_done, 2)
            link(dve.tensor_scalar(n2[:, :], ssq[:, :], 1e-24, None, ALU.max))
            rsqrt(rnorm[:, :], n2[:, :], n2h[:, :], n2t[:, :])
            dve.tensor_tensor(rqt[:, :], rnorm[:, 0:1], pars[0:C, P_TEMP:P_TEMP + 1], ALU.mult).then_inc(rnorm_done, 1)
            dve.wait_ge(rnorm_done, 1)
            dve.wait_ge(rk_spread, 1)
            link(dve.tensor_tensor(rk_blk[:, :], bank(1, cols=C), cst[0:C, K_BLK:K_BLK + C], ALU.mult))
            dve.wait_ge(score_done, 1)
            link(dve.scalar_tensor_tensor(sc_blk[:, :], bank(0, cols=C), rqt[:, 0:1], rk_blk[:, :], ALU.mult, ALU.mult))
            link(dve.tensor_reduce(sc[:, :], sc_blk[:, :].rearrange("p (h d) -> p d h", d=DH), AX.X, ALU.add))
            dve.tensor_reduce(nmax[:, :], sc[:, :], AX.X, ALU.max, negate=True).then_inc(nmax_done, 1)
            other = sc[:, :].unsqueeze(1).broadcast_to([C, DH, DH])
            own = sc[:, :].unsqueeze(2).broadcast_to([C, DH, DH])
            sq3 = lambda t: t[:, :].rearrange("p (i j) -> p i j", j=DH)
            dve.tensor_tensor(sq3(above), other, own, ALU.is_gt)
            link(dve.tensor_tensor(sq3(equal), other, own, ALU.is_equal))
            link(dve.tensor_tensor(equal[:, :], equal[:, :], cst[0:C, K_TRI:K_TRI + DH * DH], ALU.mult))
            link(dve.tensor_tensor(above[:, :], above[:, :], equal[:, :], ALU.add))
            link(dve.tensor_reduce(rank[:, :], sq3(above), AX.X, ALU.add))
            dve.wait_ge(exp_done, 1)
            for i, k in enumerate(KEEP):
                ins = dve.scalar_tensor_tensor(kept[:, i * DH:(i + 1) * DH], rank[:, :], float(k), ex[:, :],
                                               ALU.is_lt, ALU.mult, accum_out=ksum[:, i:i + 1])
            link(ins)
            link(dve.reciprocal(coef[:, :], ksum[:, :]))
            link(dve.tensor_tensor(coef[:, :], coef[:, :], pars[0:C, P_A:P_A + 4], ALU.mult))
            link(dve.tensor_scalar(att[:, :], kept[:, 0:DH], coef[:, 0:1], None, ALU.mult))
            for i in range(1, 4):
                link(dve.scalar_tensor_tensor(att[:, :], kept[:, i * DH:(i + 1) * DH], coef[:, i:i + 1], att[:, :],
                                              ALU.mult, ALU.add))
            dve.tensor_tensor(att_blk[:, :].rearrange("p (h d) -> p h d", d=DH),
                              att[:, :].unsqueeze(1).broadcast_to([C, HEADS, DH]),
                              cst[0:C, K_BLK:K_BLK + C].rearrange("p (h d) -> p h d", d=DH),
                              ALU.mult).then_inc(att_ready, 1)
            dve.wait_ge(attT_done, 1)
            dve.tensor_copy(attT[:, :], bank(4, cols=C)).then_inc(attT_copied, 1)
            for b in range(2):
                dve.wait_ge(proj_ready, b + 1)
                xv = xs[:, b * TOK // 2:(b + 1) * TOK // 2].rearrange("p (a y b x) -> p y a b x", y=2, b=POOL, x=2)
                pv = grid(pr[:, b * HP:(b + 1) * HP]).unsqueeze(3).broadcast_to([C, POOL // 2, POOL, 2])
                for y in range(2):
                    dve.tensor_tensor(xv[:, y], xv[:, y], pv, ALU.add).then_inc(x2_ready, 1)
            ln_vector(1, 1e-5, (6, 7))
            g3 = lambda t: t[:, :].rearrange("p (t e) -> p t e", e=E)
            per_e = lambda t: t[:, :].unsqueeze(2).broadcast_to([128, NT, E])
            dve.wait_ge(gscore_done, 1)
            link(dve.tensor_reduce(gm[:, :], bank(4, 128, NT * E).rearrange("p (t e) -> p t e", e=E), AX.X, ALU.max))
            dve.tensor_tensor(g3(gs), bank(4, 128, NT * E).rearrange("p (t e) -> p t e", e=E), per_e(gm),
                              ALU.subtract).then_inc(gsub_done, 1)

            def gate_steps():
                dve.wait_ge(gexp_done, 1)
                link(dve.tensor_reduce(gm[:, :], g3(ge), AX.X, ALU.add))
                link(dve.reciprocal(gm[:, :], gm[:, :]))
                link(dve.tensor_tensor(g3(gs), g3(ge), per_e(gm), ALU.mult))
                g4 = lambda t: t[:, :].rearrange("p (t i j) -> p t i j", i=E, j=E)
                gother = g3(gs).unsqueeze(2).broadcast_to([128, NT, E, E])
                gown = g3(gs).unsqueeze(3).broadcast_to([128, NT, E, E])
                tri = cst[:, K_TRIE:K_TRIE + E * E].unsqueeze(1).broadcast_to([128, NT, E * E])
                dve.tensor_tensor(g4(gcmp), gother, gown, ALU.is_gt)
                link(dve.tensor_tensor(g4(geq), gother, gown, ALU.is_equal))
                g16 = lambda t: t[:, :].rearrange("p (t i) -> p t i", i=E * E)
                link(dve.tensor_tensor(g16(geq), g16(geq), tri, ALU.mult))
                link(dve.tensor_tensor(gcmp[:, :], gcmp[:, :], geq[:, :], ALU.add))
                link(dve.tensor_reduce(grank[:, :], g4(gcmp), AX.X, ALU.add))
                link(dve.scalar_tensor_tensor(gate[:, :], grank[:, :], 2.0, gs[:, :], ALU.is_lt, ALU.mult))
                link(dve.tensor_reduce(gm[:, :], g3(gate), AX.X, ALU.add))
                link(dve.tensor_scalar(gm[:, :], gm[:, :], 1e-9, None, ALU.add))
                link(dve.reciprocal(gm[:, :], gm[:, :]))
                link(dve.tensor_tensor(g3(gate), g3(gate), per_e(gm), ALU.mult))
                part = gparts[:, :].rearrange("p (t k e) -> p t k e", k=3, e=E)
                link(dve.tensor_copy(part[:, :, 0], g3(gate)))
                link(dve.tensor_tensor(g3(gs), g3(gate), part[:, :, 0], ALU.subtract))
                link(dve.tensor_copy(part[:, :, 1], g3(gs)))
                dve.tensor_tensor(part[:, :, 2], g3(gs), part[:, :, 1], ALU.subtract).then_inc(gparts_done, 1)

            def outputs(c, q):
                for e in range(E):
                    if last_pair(e) == q:
                        dve.wait_ge(l2_done, c * NH + (e + 1) * HT)
                        dve.wait_ge(gb_copied, c * E + e + 1)
                        if not (isinstance(c, int) and c == 0 and e < 2):
                            dve.wait_ge(acc_done, c * E + e - 1)
                        dve.scalar_tensor_tensor(cols(yg, e % 2), bank(4 + e % 2, cols=CH),
                                                 pars[0:C, P_B2 + e:P_B2 + e + 1], cols(gb, e % 2),
                                                 ALU.add, ALU.mult).then_inc(y_gated, 1)

            def chunk(c, first=False):
                for p in range(NPAIR):
                    n = c * NPAIR + p
                    dve.wait_ge(gelu_done, n + 1)
                    if not (first and p < HB):
                        dve.wait_ge(l2_done, 2 * (n - HB + 1))
                    h = cols(hf, p % 2, 2 * CH)
                    hi, lo = cols(h_hi, p % HB, 2 * CH), cols(h_lo, p % HB, 2 * CH)
                    dve.tensor_copy(hi, h).then_inc(h_split, 1)
                    dve.wait_ge(h_split, 2 * n + 1)
                    dve.tensor_tensor(lo, h, hi.bitcast(F32), ALU.subtract).then_inc(h_split, 1)
                    if first and p == 0:
                        gate_steps()
                    if p >= LAG:
                        outputs(c, p - LAG)
                    elif not first:
                        outputs(c - 1, p - LAG + NPAIR)

            chunk(0, True)
            with dve.Fori(1, NCH) as c:
                chunk(c)
            for q in range(NPAIR - LAG, NPAIR):
                outputs(NCH - 1, q)

        @block.tensor
        def _(pe):
            def ln_tensor(i, src_ready, centre_banks, spread_banks):
                s = ln[i]

                def spread(c):
                    if c >= 2:
                        pe.wait_ge(s["xn"], c - 1)
                    for t in range(TPC):
                        k = c * TPC + t
                        o = bank(spread_banks[c % 2], cols=128, at=t * 128)
                        pe.matmul(o, rs_hi[:, k:k + 1].broadcast_to([128, C]), ident_r[:, :], start=(t == 0), stop=False, skip_group_check=True)
                        ins = pe.matmul(o, rs_lo[:, k:k + 1].broadcast_to([128, C]), ident_r[:, :], start=False, stop=True, skip_group_check=True)
                    ins.then_inc(s["spread"], 1)

                def stats(c):
                    pe.wait_ge(s["sq"], c + 1)
                    for t in range(TPC):
                        k = c * TPC + t
                        ins = pe.matmul(bank(2 + c // HALF, 128, 1, at=k % (HALF * TPC)),
                                        sq[:, k * 128:(k + 1) * 128], mean_w[:, :], start=True, stop=True)
                    if c % HALF == HALF - 1:
                        ins.then_inc(s["var"], 1)

                for c in range(NCH):
                    src_ready(c)
                    if c >= 2:
                        pe.wait_ge(s["sq"], c - 1)
                    pe.matmul(bank(centre_banks[c % 2], cols=CH), cst[0:C, K_CEN:K_CEN + C], cols(xs, c),
                              start=True, stop=True).then_inc(s["centred"], 1)
                    if c >= 1:
                        stats(c - 1)
                    if c == HALF + 1:
                        pe.wait_ge(s["rstd"], 1)
                        for cc in range(2):
                            spread(cc)
                stats(NCH - 1)
                spread(2)
                pe.wait_ge(s["rstd"], 2)
                for c in range(HALF, NCH):
                    spread(c)

            pe.wait_ge(cst_in, 16)
            pe.wait_ge(par_in, 16)
            pe.wait_ge(ones_set, 3)
            pe.wait_ge(rows_set, 2)
            pe.wait_ge(ident_set, 2)
            ln_tensor(0, lambda c: pe.wait_ge(x_in[c // 2], 16), (0, 1), (4, 5))
            n = 0
            for g in (1, 0, 2):
                for c in range(NCH):
                    if n < NCH:
                        pe.wait_ge(ln[0]["xn"], c + 1)
                    if n >= 4:
                        pe.wait_ge(pool_done, n - 3)
                    pe.matmul(bank((6, 7, 0, 1)[n % 4], cols=CH), pars[:, P_QKV + g * C:P_QKV + (g + 1) * C],
                              cols(xn, c), start=True, stop=True).then_inc(qkv_done, 1)
                    n += 1
            pe.wait_ge(pool_done, 18)
            pe.wait_ge(diag_set, 9)
            for b in range(2):
                for t in range(9):
                    ins = pe.matmul(bank(2 + b, cols=HP), diag[:, t * C:(t + 1) * C],
                                    tap(2, t, b * POOL // 2, POOL // 2), start=(t == 0), stop=(t == 8))
                ins.then_inc(vconv_done, 1)
            for n, g in enumerate((1, 0)):
                pe.wait_ge(conv_done, n + 1)
                for b in range(2):
                    for t in range(TB // 2):
                        j = b * (TB // 2) + t
                        ins = pe.transpose(bank(4 + 2 * g + b, cols=C, at=t * C),
                                           qkc[:, g * PIX + j * C:g * PIX + (j + 1) * C], ident[0:C, 0:C])
                    ins.then_inc(qkT_done, 1)
            pe.wait_ge(qkT_copied, 4)
            for j in range(TB):
                ins = pe.matmul(bank(0, cols=C), qkT[:, j * C:(j + 1) * C], qkT[:, PIX + j * C:PIX + (j + 1) * C],
                                start=(j == 0), stop=(j == TB - 1))
            ins.then_inc(score_done, 1)
            pe.wait_ge(rnorm_done, 1)
            pe.matmul(bank(1, cols=C), rnorm[:, 1:2].broadcast_to([C, C]), ident[0:C, 0:C],
                      start=True, stop=True).then_inc(rk_spread, 1)
            pe.wait_ge(att_ready, 1)
            pe.transpose(bank(4, cols=C), att_blk[:, :], ident[0:C, 0:C]).then_inc(attT_done, 1)
            pe.wait_ge(attT_copied, 1)
            pe.wait_ge(v_ready, 2)
            for b in range(2):
                pe.matmul(bank(6 + b, cols=HP), attT[:, :], vc[:, b * HP:(b + 1) * HP],
                          start=True, stop=True).then_inc(av_done, 1)
            for b in range(2):
                pe.wait_ge(gelu_o, b + 1)
                pe.matmul(bank(b, cols=HP), pars[0:C, P_PROJ:P_PROJ + C], go[:, b * HP:(b + 1) * HP],
                          start=True, stop=True).then_inc(proj_done, 1)
            ln_tensor(1, lambda c: pe.wait_ge(x2_ready, 2 * (c // HALF + 1)), (4, 5), (6, 7))
            pe.wait_ge(ln[1]["xn"], NCH)
            for k in range(NT):
                ins = pe.matmul(bank(4, 128, E, at=k * E), xn[:, k * 128:(k + 1) * 128],
                                pars[:, P_GATE:P_GATE + E], start=True, stop=True)
            ins.then_inc(gscore_done, 1)
            pe.wait_ge(w_split, 4)
            pe.wait_ge(split_lo, NCH)

            def first_product(c, p):
                for j in (2 * p, 2 * p + 1):
                    o = bank(2 * (p % 2) + j % 2, 128, CH)
                    w = slice(j * 128, (j + 1) * 128)
                    pe.matmul(o, w1_hi[:, w], cols(xn_hi, c), start=True, stop=False)
                    pe.matmul(o, w1_hi[:, w], cols(xn_lo, c), start=False, stop=False)
                    ins = pe.matmul(o, w1_lo[:, w], cols(xn_hi, c), start=False, stop=True)
                ins.then_inc(l1_done, 1)

            def second_product(c, q):
                for e in range(E):
                    if last_pair(e) - 1 == q:
                        if not (isinstance(c, int) and c == 0 and e < 2):
                            pe.wait_ge(gb_copied, c * E + e - 1)
                        pe.matmul(bank(6 + e % 2, cols=CH), sel_b[:, e * C:(e + 1) * C], cols(gateT, c),
                                  start=True, stop=True).then_inc(gb_done, 1)
                pe.wait_ge(h_split, 2 * (c * NPAIR + q + 1))
                for j in (2 * q, 2 * q + 1):
                    e, t = divmod(j, HT)
                    if t == 0 and not (isinstance(c, int) and c == 0 and e < 2):
                        pe.wait_ge(y_gated, c * E + e - 1)
                    o = bank(4 + e % 2, cols=CH)
                    w = slice(j * C, (j + 1) * C)
                    at = (q % HB) * 2 * CH + (j % 2) * CH
                    pe.matmul(o, w2_hi[:, w], h_hi[:, at:at + CH], start=(t == 0), stop=False)
                    pe.matmul(o, w2_hi[:, w], h_lo[:, at:at + CH], start=False, stop=False)
                    ins = pe.matmul(o, w2_lo[:, w], h_hi[:, at:at + CH], start=False, stop=(t == HT - 1))
                    ins.then_inc(l2_done, 1)

            def chunk(c, first=False):
                for p in range(NPAIR):
                    if not (first and p < 2):
                        pe.wait_ge(gelu_done, c * NPAIR + p - 1)
                    first_product(c, p)
                    if first and p == 0:
                        pe.wait_ge(gparts_done, 1)
                        for b in range(3):
                            if b == 2:
                                pe.wait_ge(gT_copied, 1)
                            dst = psum[0:3 * E, (6 + b % 2) * BANK:(6 + b % 2) * BANK + 384].bitcast(BF16)
                            for t in range(6):
                                k = b * 6 + t
                                ins = pe.transpose(dst[:, t * 128:(t + 1) * 128],
                                                   gparts[:, k * 3 * E:(k + 1) * 3 * E], ident_b[:, :])
                            ins.then_inc(gT_done, 1)
                    if first and p == LAG:
                        pe.wait_ge(gT_copied, 3)
                    if p >= LAG:
                        second_product(c, p - LAG)
                    elif not first:
                        second_product(c - 1, p - LAG + NPAIR)

            pe.wait_ge(sel_set, 1)
            pe.wait_ge(gsub_done, 1)
            chunk(0, True)
            with pe.Fori(1, NCH) as c:
                chunk(c)
            for q in range(NPAIR - LAG, NPAIR):
                second_product(NCH - 1, q)


def _constants():
    import numpy as np
    k = np.zeros((128, K_END), np.float32)
    k[:, K_ID:K_ID + 128] = np.eye(128)
    k[:C, K_CEN:K_CEN + C] = np.eye(C) - 1.0 / C
    k[:C, K_BLK:K_BLK + C] = np.kron(np.eye(HEADS), np.ones((DH, DH)))
    k[:, K_TRI:K_TRI + DH * DH] = np.tril(np.ones((DH, DH)), -1).reshape(-1)
    k[:, K_TRIE:K_TRIE + E * E] = np.tril(np.ones((E, E)), -1).reshape(-1)
    k[:3 * E, K_SEL:K_SEL + E * C] = np.tile(np.repeat(np.eye(E), C, axis=1), (3, 1))
    return k


def kernel(x, L0_conv_w_qkv, L0_conv_b_qkv, L0_conv_w_dw, L0_conv_b_dw, L0_conv_w_proj, L0_conv_b_proj,
           L0_conv_temperature, L0_conv_a1, L0_conv_a2, L0_conv_a3, L0_conv_a4,
           L0_ffn_gate_w, L0_ffn_gate_b, L0_ffn_w1, L0_ffn_b1, L0_ffn_w2, L0_ffn_b2):
    import numpy as np
    import concourse.bacc as bacc
    from concourse import mybir as mb
    from concourse.bass_utils import run_bass_kernel_spmd as run

    f = lambda a: np.ascontiguousarray(np.asarray(a))
    par = np.zeros((C + 1, P_END), np.float32)
    par[:C, P_QKV:P_QKV + 3 * C] = f(L0_conv_w_qkv).T
    par[C, P_QKV:P_QKV + 3 * C] = f(L0_conv_b_qkv)
    par[:C, P_PROJ:P_PROJ + C] = f(L0_conv_w_proj).T
    par[:C, P_GATE:P_GATE + E] = f(L0_ffn_gate_w)
    par[C, P_GATE:P_GATE + E] = f(L0_ffn_gate_b)
    par[:C, P_DW:P_DW + 27] = f(L0_conv_w_dw).reshape(3, C, 9).transpose(1, 0, 2).reshape(C, 27)
    par[:C, P_BDW:P_BDW + 3] = f(L0_conv_b_dw).reshape(3, C).T
    par[:C, P_BPROJ] = f(L0_conv_b_proj)
    par[:C, P_TEMP] = np.repeat(f(L0_conv_temperature).reshape(-1), DH)
    for i, a in enumerate((L0_conv_a1, L0_conv_a2, L0_conv_a3, L0_conv_a4)):
        par[:C, P_A + i] = f(a)[0]
    par[:C, P_B2:P_B2 + E] = f(L0_ffn_b2).T
    arrays = {
        "x": f(x).reshape(C, TOK),
        "par": par,
        "b1": f(L0_ffn_b1).reshape(1, E * HID),
        "w1": f(L0_ffn_w1),
        "w2": f(L0_ffn_w2),
        "consts": _constants(),
    }
    nc = bacc.Bacc("TRN2", target_bir_lowering=False, num_devices=1)
    args = [nc.dram_tensor(n, a.shape, mb.dt.float32, kind="ExternalInput").ap() for n, a in arrays.items()]
    out = nc.dram_tensor("out", (C, TOK), mb.dt.float32, kind="ExternalOutput").ap()
    build(nc, *args, out)
    r = run(nc, [arrays], core_ids=[0])
    return r.results[0]["out"].reshape(1, C, IMG, IMG)
```

```python
import concourse.bass as bass
from concourse import mybir
from contextlib import ExitStack

F32 = mybir.dt.float32
F32R = mybir.dt.float32r
BF16 = mybir.dt.bfloat16
I32 = mybir.dt.int32
ALU = mybir.AluOpType
ACT = mybir.ActivationFunctionType
AX = mybir.AxisListType

C = 96
IMG = 48
TOK = IMG * IMG
POOL = IMG // 2
PIX = POOL * POOL
PAD = POOL + 2
HEADS = 8
DH = C // HEADS
KEEP = (DH // 2, DH * 2 // 3, DH * 3 // 4, DH * 4 // 5)
E = 4
HID = 4 * C
HT = HID // 128
NH = E * HT
CH = 384
NCH = TOK // CH
TPC = CH // 128
NT = TOK // 128
HALF = NCH // 2
NPAIR = NH // 2
LAG = 2
IDLE = (18, 2, 0, 4, 8, 4, 4, 4)
BY_SCALAR = (1, 4)
QKV_BANKS = (0, 1, 2, 3, 6, 7)
TURN_AT = 5
HB = 3
BANK = 512
TB = PIX // C
HP = PIX // 2

P_QKV = 0
P_PROJ = P_QKV + 3 * C
P_GATE = P_PROJ + C
P_DW = P_GATE + E
P_SPLIT = P_DW + 27
P_BDW = P_SPLIT
P_BPROJ = P_BDW + 3
P_TEMP = P_BPROJ + 1
P_A = P_TEMP + 1
P_B2 = P_A + 4
P_END = P_B2 + E

K_ID = 0
K_BLK = K_ID + 128
K_TRI = K_BLK + C
K_TRIE = K_TRI + DH * DH
K_END = K_TRIE + E * E


QKV_ORDER = [(g, c) for half in range(2) for g in (2, 1, 0) for c in range(half * HALF, (half + 1) * HALF)]


def finished(q, first):
    if first:
        return {3: (0, 1), 4: (2,), 5: (3,)}.get(q, ())
    return tuple(e for e in range(E) if (HT * e + HT - 1) // 2 == q)


def build(nc, x, xt, par, b1, w1, w2, const, sel, out):
    ctx = ExitStack()
    with ctx:
        def sb(name, shape, dt=F32):
            return ctx.enter_context(nc.sbuf_tensor(name, shape, dt))

        def sem(name):
            return ctx.enter_context(nc.semaphore(name))

        psum = ctx.enter_context(nc.psum_tensor("psum", [128, 8 * BANK], F32))

        def bank(b, rows=C, cols=BANK, at=0):
            return psum[0:rows, b * BANK + at:b * BANK + at + cols]

        xs = sb("xs", [C, TOK])
        pars = sb("pars", [C + 1, P_END])
        cst = sb("cst", [128, K_END])
        ident = cst[:, K_ID:K_ID + 128]
        ident_b = sb("ident_b", [128, 128], BF16)
        sel_b = sb("sel_b", [128, E * C], BF16)
        sels = sb("sels", [3 * E, E * C])
        gate_r = sb("gate_r", [C + 1, 2 * E], F32R)
        w1s = sb("w1s", [C + 1, E * HID])
        w1_hi = sb("w1_hi", [C + 1, E * HID], F32R)
        w1_lo = sb("w1_lo", [C + 1, E * HID], F32R)
        w2s = sb("w2s", [128, NH * C])
        w2_hi = sb("w2_hi", [128, NH * C], F32R)
        w2_lo = sb("w2_lo", [128, NH * C], F32R)
        xT = sb("xT", [128, NT * C])
        xnT = sb("xnT", [128, NT * C])
        stats = sb("stats", [128, NT * 6])
        mv = sb("mv", [128, NT * 2])
        xn = sb("xn", [C, TOK])
        xn_hi = sb("xn_hi", [C + 1, TOK], F32R)
        xn_lo = sb("xn_lo", [C + 1, TOK], F32R)
        var = sb("var", [128, NT])
        seed = sb("seed", [128, NT])
        nhalf = sb("nhalf", [128, NT])
        newton = sb("newton", [128, NT])
        newton2 = sb("newton2", [128, NT])
        nmr = sb("nmr", [128, NT])
        pooled = sb("pooled", [C, 3 * PAD * PAD])
        qkc = sb("qkc", [C, 2 * PIX])
        qkT = sb("qkT", [C, 2 * PIX])
        vc = sb("vc", [C, PIX])
        par_hi = sb("par_hi", [C + 1, P_SPLIT], F32R)
        par_lo = sb("par_lo", [C + 1, P_SPLIT], F32R)
        diag_hi = sb("diag_hi", [C, 9 * C], F32R)
        diag_lo = sb("diag_lo", [C, 9 * C], F32R)
        kp_hi = sb("kp_hi", [C, PAD * PAD], F32R)
        kp_lo = sb("kp_lo", [C, PAD * PAD], F32R)
        idle_b = sb("idle_b", [128, BANK], BF16)
        sqj = sb("sqj", [C, PIX])
        ssq = sb("ssq", [C, 2])
        n2 = sb("n2", [C, 2])
        n2h = sb("n2h", [C, 2])
        n2t = sb("n2t", [C, 2])
        n2u = sb("n2u", [C, 2])
        rnorm = sb("rnorm", [C, 2])
        rqt = sb("rqt", [C, 1])
        rk_blk = sb("rk_blk", [C, C])
        sc_blk = sb("sc_blk", [C, C])
        sc = sb("sc", [C, DH])
        nmax = sb("nmax", [C, 1])
        ex = sb("ex", [C, DH])
        above = sb("above", [C, DH * DH])
        equal = sb("equal", [C, DH * DH])
        rank = sb("rank", [C, DH])
        kept = sb("kept", [C, 4 * DH])
        ksum = sb("ksum", [C, 4])
        coef = sb("coef", [C, 4])
        scaled = sb("scaled", [C, 4 * DH])
        att = sb("att", [C, DH])
        att_blk = sb("att_blk", [C, C])
        attT = sb("attT", [C, C])
        go = sb("go", [C, PIX])
        pr = sb("pr", [C, PIX])
        g8 = sb("g8", [128, NT * 2 * E])
        vprod = sb("vprod", [C, 2 * PIX])
        gs = sb("gs", [128, NT * E])
        gm = sb("gm", [128, NT])
        ge = sb("ge", [128, NT * E])
        gcmp = sb("gcmp", [128, NT * E * E])
        grank = sb("grank", [128, NT * E])
        gate = sb("gate", [128, NT * E])
        gparts = sb("gparts", [128, NT * 3 * E], BF16)
        gateT = sb("gateT", [128, TOK], BF16)
        gb = sb("gb", [C, 2 * CH])
        hf = sb("hf", [128, 2 * 2 * CH])
        h_hi = sb("h_hi", [128, HB * 2 * CH], F32R)
        h_lo = sb("h_lo", [128, HB * 2 * CH], F32R)
        yg = sb("yg", [C, 2 * CH])

        x_in = sem("x_in")
        xt_in = [sem(f"xt_in{i}") for i in range(2)]
        sel_in = sem("sel_in")
        par_in, cst_in, w1_in, w2_in = sem("par_in"), sem("cst_in"), sem("w1_in"), sem("w2_in")
        ones_set = sem("ones_set")
        idle_set = sem("idle_set")
        par_split = sem("par_split")
        kp_split = sem("kp_split")
        lastrow_set = sem("lastrow_set")
        ident_set = sem("ident_set")
        diag_set = sem("diag_set")
        sel_set = sem("sel_set")
        w_split = sem("w_split")
        dve_chain = sem("dve_chain")
        ln = [{n: sem(f"ln{i}_{n}") for n in
               ("stats", "rstd", "by_vector", "by_scalar", "turned", "hi", "lo")} for i in range(2)]
        x2T_done = sem("x2T_done")
        gate_split = sem("gate_split")
        qkv_done, pool_done = sem("qkv_done"), sem("pool_done")
        kconv_done, k_ready = sem("kconv_done"), sem("k_ready")
        qtap_done, qconv_done = sem("qtap_done"), sem("qconv_done")
        vprod_done, v_ready = sem("vprod_done"), sem("v_ready")
        ssq_done, rnorm_done = sem("ssq_done"), sem("rnorm_done")
        qkT_done, qkT_copied = sem("qkT_done"), sem("qkT_copied")
        rk_spread, score_done = sem("rk_spread"), sem("score_done")
        nmax_done, exp_done = sem("nmax_done"), sem("exp_done")
        att_ready, attT_done, attT_copied = sem("att_ready"), sem("attT_done"), sem("attT_copied")
        av_done, gelu_o, proj_done, proj_ready = sem("av_done"), sem("gelu_o"), sem("proj_done"), sem("proj_ready")
        x2_ready = [sem("x2_ready_vector"), sem("x2_ready_gpsimd")]
        gscore_done, gscore_copied, gsub_done, gexp_done, gparts_done = (
            sem("gscore_done"), sem("gscore_copied"), sem("gsub_done"), sem("gexp_done"), sem("gparts_done"))
        gT_done, gT_copied = sem("gT_done"), sem("gT_copied")
        l1_done, gelu_done, h_split, l2_done = sem("l1_done"), sem("gelu_done"), sem("h_split"), sem("l2_done")
        gb_done, gb_copied, y_gated, acc_done = sem("gb_done"), sem("gb_copied"), sem("y_gated"), sem("acc_done")
        out_done = sem("out_done")

        block = ctx.enter_context(nc.Block())

        def padded(g):
            return pooled[:, g * PAD * PAD:(g + 1) * PAD * PAD].rearrange("p (a b) -> p a b", b=PAD)

        def tap(g, t, r0=0, rows=POOL):
            dy, dx = divmod(t, 3)
            return padded(g)[:, r0 + dy:r0 + dy + rows, dx:dx + POOL]

        def grid(ap):
            return ap.rearrange("p (a b) -> p a b", b=POOL)

        def turn_bank(i, c):
            return c % 2 if i == 1 and c < HALF else 4 + c % 2

        def tap_of(t, ap, b):
            dy, dx = divmod(t, 3)
            r = b * POOL // 2 + dy
            return ap[:, :].rearrange("p (a b) -> p a b", b=PAD)[:, r:r + POOL // 2, dx:dx + POOL]

        def x2_views(b, y):
            xv = xs[:, b * TOK // 2:(b + 1) * TOK // 2].rearrange("p (a y b x) -> p y a b x", y=2, b=POOL, x=2)
            return xv[:, y], grid(pr[:, b * HP:(b + 1) * HP]).unsqueeze(3).broadcast_to([C, POOL // 2, POOL, 2])

        def cols(ap, c, n=CH):
            return ap[:, bass.ds(c * n, n)]

        @block.sync
        def _(sp):
            hw = NT // 2 * C
            sp.dma_start(xT[:, 0:hw], xt[:, 0:hw]).then_inc(xt_in[0], 16)
            sp.dma_start(pars[:, :], par).then_inc(par_in, 16)
            sp.dma_start(w1s[0:C, :].rearrange("p (e h) -> p e h", e=E),
                         w1.rearrange("e d h -> d e h")).then_inc(w1_in, 16)
            sp.dma_start(w1s[C:C + 1, :], b1).then_inc(w1_in, 16)
            sp.dma_start(w2s[:, :].rearrange("p (j d) -> p j d", d=C),
                         w2.rearrange("e (t p) d -> p (e t) d", p=128)).then_inc(w2_in, 16)
            with sp.Fori(0, NCH) as c:
                sp.wait_ge(acc_done, c * E + E)
                sp.dma_start(out[:, bass.ds(c * CH, CH)], cols(xs, c)).then_inc(out_done, 16)
            sp.wait_ge(out_done, 16 * NCH)

        @block.gpsimd
        def _(pool):
            def low(dst, src, hi, done):
                return pool.tensor_tensor(dst, src, hi.bitcast(F32), ALU.subtract).then_inc(done, 1)

            pool.memset(pooled[:, :], 0.0).then_inc(ones_set, 1)
            pool.wait_ge(ones_set, 1)
            pool.memset(xn_hi[C:C + 1, :].bitcast(F32), 1.0).then_inc(lastrow_set, 1)
            pool.memset(xn_lo[C:C + 1, :].bitcast(F32), 0.0).then_inc(lastrow_set, 1)
            pool.wait_ge(lastrow_set, 2)
            pool.wait_ge(par_in, 16)
            pool.wait_ge(par_split, 1)
            low(par_lo[:, :], pars[:, 0:P_SPLIT], par_hi[:, :], par_split)
            pool.wait_ge(par_split, 2)
            pool.wait_ge(cst_in, 16)

            def low_diagonal(t):
                w = P_DW + 9 + t
                pool.tensor_scalar(diag_lo[:, t * C:(t + 1) * C], ident[0:C, 0:C],
                                   par_lo[0:C, w:w + 1].bitcast(F32), None, ALU.mult).then_inc(diag_set, 1)

            for t in range(5):
                low_diagonal(t)
            for c in range(NCH):
                pool.wait_ge(ln[0]["hi"], c + 1)
                low(cols(xn_lo, c)[0:C], cols(xn, c), cols(xn_hi, c)[0:C], ln[0]["lo"])
            for t in range(5, 9):
                low_diagonal(t)
            pool.wait_ge(kp_split, 1)
            low(kp_lo[:, :], pooled[:, PAD * PAD:2 * PAD * PAD], kp_hi[:, :], kp_split)
            for t in range(1, 9):
                pool.wait_ge(vprod_done, t + 1)
                if t >= 2:
                    pool.wait_ge(v_ready, t - 1)
                pool.tensor_tensor(vc[:, :], vc[:, :], vprod[:, (t % 2) * PIX:(t % 2 + 1) * PIX],
                                   ALU.add).then_inc(v_ready, 1)
            pool.wait_ge(w_split, 2)
            low(w1_lo[:, :], w1s[:, :], w1_hi[:, :], w_split)
            pool.wait_ge(w_split, 3)
            low(w2_lo[:, :], w2s[:, :], w2_hi[:, :], w_split)
            pool.wait_ge(w_split, 4)
            pool.wait_ge(gate_split, 1)
            low(gate_r[:, E:2 * E], pars[:, P_GATE:P_GATE + E], gate_r[:, 0:E], gate_split)
            pool.wait_ge(gate_split, 2)
            pool.wait_ge(x_in, 16)
            pool.wait_ge(proj_ready, 2)
            for y in range(2):
                xv, pv = x2_views(1, y)
                pool.tensor_tensor(xv, xv, pv, ALU.add).then_inc(x2_ready[1], 1)
            for c in range(NCH):
                pool.wait_ge(ln[1]["hi"], c + 1)
                low(cols(xn_lo, c)[0:C], cols(xn, c), cols(xn_hi, c)[0:C], ln[1]["lo"])
            pool.wait_ge(ln[1]["lo"], NCH)
            pool.memset(gateT[:, :].bitcast(F32), 0.0).then_inc(ones_set, 1)
            pool.memset(sel_b[:, :].bitcast(F32), 0.0).then_inc(sel_set, 1)
            pool.wait_ge(sel_set, 1)
            pool.wait_ge(ones_set, 2)
            pool.wait_ge(sel_in, 16)
            pool.tensor_copy(sel_b[0:3 * E, :], sels[:, :]).then_inc(sel_set, 1)
            pool.wait_ge(sel_set, 2)
            for c in range(NCH):
                for e in range(E):
                    pool.wait_ge(y_gated, c * E + e + 1)
                    if e:
                        pool.wait_ge(acc_done, c * E + e)
                    pool.tensor_tensor(cols(xs, c), cols(xs, c), cols(yg, e % 2), ALU.add).then_inc(acc_done, 1)

        @block.scalar
        def _(act):
            hw = NT // 2 * C
            act.dma_start(cst[:, :], const).then_inc(cst_in, 16)
            act.dma_start(xT[:, hw:], xt[:, hw:]).then_inc(xt_in[1], 16)
            act.dma_start(sels[:, :], sel).then_inc(sel_in, 16)
            act.dma_start(xs[:, :], x).then_inc(x_in, 16)
            act.wait_ge(cst_in, 16)
            act.activation(ident_b[:, :], ident, ACT.Copy).then_inc(ident_set, 1)
            act.wait_ge(par_in, 16)
            act.activation(par_hi[:, :], pars[:, 0:P_SPLIT], ACT.Copy).then_inc(par_split, 1)
            act.activation(gate_r[:, 0:E], pars[:, P_GATE:P_GATE + E], ACT.Copy).then_inc(gate_split, 1)

            for t in range(9):
                w = P_DW + 9 + t
                act.activation(diag_hi[:, t * C:(t + 1) * C], ident[0:C, 0:C], ACT.Copy,
                               scale=pars[0:C, w:w + 1]).then_inc(diag_set, 1)

            def normalise(i, c, src):
                act.wait_ge(ln[i]["rstd"], c // HALF + 1)
                for k in range(c * TPC, (c + 1) * TPC):
                    act.activation(xnT[:, k * C:(k + 1) * C], src(k), ACT.Identity, scale=seed[:, k:k + 1],
                                   bias=nmr[:, k:k + 1]).then_inc(ln[i]["by_scalar"], 1)

            def take(i, c):
                act.wait_ge(ln[i]["turned"], c + 1)
                act.activation(cols(xn_hi, c)[0:C], bank(turn_bank(i, c), cols=CH), ACT.Copy)
                act.activation(cols(xn, c), bank(turn_bank(i, c), cols=CH), ACT.Copy).then_inc(ln[i]["hi"], 1)

            for half in range(2):
                normalise(0, BY_SCALAR[half], lambda k: xT[:, k * C:(k + 1) * C])
                for c in range(half * HALF, (half + 1) * HALF):
                    take(0, c)
            act.wait_ge(w1_in, 32)
            act.activation(w1_hi[:, :], w1s[:, :], ACT.Copy).then_inc(w_split, 1)
            act.wait_ge(w2_in, 16)
            act.activation(w2_hi[:, :], w2s[:, :], ACT.Copy).then_inc(w_split, 1)

            def v_product(t):
                w = pars[0:C, P_DW + 18 + t:P_DW + 19 + t]
                if t == 0:
                    act.activation(grid(vc[:, :]), tap(2, t), ACT.Identity, scale=w,
                                   bias=pars[0:C, P_BDW + 2:P_BDW + 3]).then_inc(vprod_done, 1)
                else:
                    if t >= 3:
                        act.wait_ge(v_ready, t - 2)
                    act.activation(grid(vprod[:, (t % 2) * PIX:(t % 2 + 1) * PIX]), tap(2, t), ACT.Copy,
                                   scale=w).then_inc(vprod_done, 1)

            act.wait_ge(pool_done, 12)
            v_product(0)
            v_product(1)
            act.wait_ge(pool_done, 15)
            act.activation(kp_hi[:, :], pooled[:, PAD * PAD:2 * PAD * PAD], ACT.Copy).then_inc(kp_split, 1)
            for t in range(2, 7):
                v_product(t)
            for b in range(2):
                act.wait_ge(kconv_done, b + 1)
                act.activation(qkc[:, PIX + b * HP:PIX + (b + 1) * HP], bank(2 + b, cols=HP), ACT.Identity,
                               bias=pars[0:C, P_BDW + 1:P_BDW + 2]).then_inc(k_ready, 1)
            act.wait_ge(k_ready, 2)
            act.activation(sqj[:, :], qkc[:, PIX:], ACT.Square, accum_out=ssq[:, 1:2]).then_inc(ssq_done, 1)
            act.wait_ge(ssq_done, 1)
            act.wait_ge(qconv_done, 2)
            act.activation(sqj[:, :], qkc[:, 0:PIX], ACT.Square, accum_out=ssq[:, 0:1]).then_inc(ssq_done, 1)
            for g in (1, 0):
                for b in range(2):
                    act.wait_ge(qkT_done, 2 * (1 - g) + b + 1)
                    act.activation(qkT[:, g * PIX + b * HP:g * PIX + (b + 1) * HP],
                                   bank(4 + 2 * g + b, cols=HP), ACT.Copy).then_inc(qkT_copied, 1)
            v_product(7)
            v_product(8)
            act.wait_ge(nmax_done, 1)
            act.activation(ex[:, :], sc[:, :], ACT.Exp, bias=nmax[:, 0:1]).then_inc(exp_done, 1)
            for b in range(2):
                act.wait_ge(av_done, b + 1)
                act.activation(go[:, b * HP:(b + 1) * HP], bank(6 + b, cols=HP), ACT.Gelu).then_inc(gelu_o, 1)
            for b in range(2):
                act.wait_ge(proj_done, b + 1)
                act.activation(pr[:, b * HP:(b + 1) * HP], bank(b, cols=HP), ACT.Identity,
                               bias=pars[0:C, P_BPROJ:P_BPROJ + 1]).then_inc(proj_ready, 1)
            x2_tile = lambda k: bank(2 + k // TPC, 128, C, at=k % TPC * C)
            normalise(1, BY_SCALAR[0], x2_tile)
            for c in range(HALF):
                take(1, c)
            normalise(1, BY_SCALAR[1], x2_tile)

            def gates(c, q, first=False):
                for e in finished(q, first):
                    act.wait_ge(gb_done, c * E + e + 1)
                    if not (first and e < 2):
                        act.wait_ge(y_gated, c * E + e - 1)
                    act.activation(cols(gb, e % 2), bank(6 + e % 2, cols=CH), ACT.Copy).then_inc(gb_copied, 1)

            def chunk(c, first=False):
                for p in range(NPAIR):
                    act.wait_ge(l1_done, c * NPAIR + p + 1)
                    if not (first and p < 2):
                        act.wait_ge(h_split, 2 * (c * NPAIR + p - 1))
                    act.activation(cols(hf, p % 2, 2 * CH).rearrange("p (j n) -> p j n", n=CH),
                                   psum[:, (p % 2) * 2 * BANK:(p % 2 + 1) * 2 * BANK]
                                   .rearrange("p (j n) -> p j n", n=BANK)[:, :, 0:CH],
                                   ACT.Gelu).then_inc(gelu_done, 1)
                    if first and p == 0:
                        for d in range(HALF, NCH):
                            take(1, d)
                    if first and p == 2:
                        act.wait_ge(gscore_done, 1)
                        act.activation(g8[:, :], bank(7, 128, NT * 2 * E), ACT.Copy).then_inc(gscore_copied, 1)
                    if first and p == 3:
                        act.wait_ge(gsub_done, 1)
                        act.activation(ge[:, :], gs[:, :], ACT.Exp).then_inc(gexp_done, 1)
                    if first and p == 4:
                        act.wait_ge(ones_set, 2)
                        for b in range(3):
                            act.wait_ge(gT_done, b + 1)
                            act.activation(gateT[0:3 * E, b * 768:(b + 1) * 768],
                                           psum[0:3 * E, (6 + b % 2) * BANK:(6 + b % 2) * BANK + 384].bitcast(BF16),
                                           ACT.Copy).then_inc(gT_copied, 1)
                    if p >= LAG:
                        gates(c, p - LAG, first)
                    elif not first:
                        gates(c - 1, p - LAG + NPAIR)

            chunk(0, True)
            with act.Fori(1, NCH) as c:
                chunk(c)
            for q in range(NPAIR - LAG, NPAIR):
                gates(NCH - 1, q)

        @block.vector
        def _(dve):
            chain = [0]

            def link(ins, meanwhile=None):
                chain[0] += 1
                ins.then_inc(dve_chain, 1)
                if meanwhile:
                    meanwhile()
                dve.wait_ge(dve_chain, chain[0])

            def rsqrt(y, v, nh, t, u, meanwhile=None):
                dve.tensor_scalar(nh, v, -0.5, None, ALU.mult)
                link(dve.tensor_scalar(y.bitcast(I32), v.bitcast(I32), -0.5, 1597463007.0, ALU.mult, ALU.add),
                     meanwhile)
                link(dve.tensor_tensor(t, y, y, ALU.mult), meanwhile)
                link(dve.tensor_tensor(t, t, nh, ALU.mult), meanwhile)
                dve.scalar_tensor_tensor(y, t, 1.5, y, ALU.add, ALU.mult)
                link(dve.scalar_tensor_tensor(u, t, 1.5, t, ALU.add, ALU.mult), meanwhile)
                link(dve.scalar_tensor_tensor(t, t, 1.5, u, ALU.add, ALU.mult), meanwhile)
                link(dve.scalar_tensor_tensor(y, t, 1.5, y, ALU.add, ALU.mult), meanwhile)
                link(dve.tensor_tensor(t, y, y, ALU.mult), meanwhile)
                link(dve.tensor_tensor(t, t, nh, ALU.mult), meanwhile)
                return dve.scalar_tensor_tensor(y, t, 1.5, y, ALU.add, ALU.mult)

            def ln_vector(i, eps, src, ready):
                done = ln[i]["stats"]
                moments = mv[:, :].rearrange("p (t k) -> p t k", k=2)
                halves = [range(h * NT // 2, (h + 1) * NT // 2) for h in range(2)]
                by_vector = [[k for k in tiles if k // TPC not in BY_SCALAR] for tiles in halves]

                def statistics(k):
                    ready(k)
                    dve.bn_stats(stats[:, k * 6:(k + 1) * 6], src(k)).then_inc(done, 1)

                def normalise(k):
                    dve.tensor_scalar(xnT[:, k * C:(k + 1) * C], src(k), mv[:, 2 * k:2 * k + 1],
                                      seed[:, k:k + 1], ALU.subtract, ALU.mult).then_inc(ln[i]["by_vector"], 1)

                for k in halves[0]:
                    statistics(k)
                for half, tiles in enumerate(halves):
                    z = slice(tiles[0], tiles[-1] + 1)
                    for k in tiles:
                        dve.wait_ge(done, k + 1)
                        ins = dve.bn_aggr(mv[:, 2 * k:2 * k + 2], stats[:, k * 6:(k + 1) * 6])
                    waiting = [(statistics, k) for k in halves[1]] if half == 0 else \
                        [(normalise, k) for k in by_vector[0]]
                    steps = iter(waiting)

                    def meanwhile():
                        for work, k in steps:
                            work(k)
                            break

                    link(ins, meanwhile)
                    link(dve.tensor_scalar(var[:, z], moments[:, z, 1], eps, None, ALU.add))
                    link(rsqrt(seed[:, z], var[:, z], nhalf[:, z], newton[:, z], newton2[:, z], meanwhile))
                    dve.scalar_tensor_tensor(nmr[:, z], moments[:, z, 0], -1.0, seed[:, z], ALU.mult,
                                             ALU.mult).then_inc(ln[i]["rstd"], 1)
                for k in by_vector[1]:
                    normalise(k)

            def x_arrives(k):
                if k % (NT // 2) == 0:
                    dve.wait_ge(xt_in[k // (NT // 2)], 16)

            dve.memset(idle_b[:, :].bitcast(F32), 0.0).then_inc(idle_set, 1)
            ln_vector(0, 1e-6, lambda k: xT[:, k * C:(k + 1) * C], x_arrives)
            dve.wait_ge(ones_set, 1)
            for n, (g, c) in enumerate(QKV_ORDER):
                dve.wait_ge(qkv_done, n + 1)
                src = bank(QKV_BANKS[n % 6], cols=CH).rearrange("p (a y b x) -> p a b y x", y=2, b=POOL, x=2)
                dve.tensor_reduce(padded(g)[:, 1 + 4 * c:5 + 4 * c, 1:1 + POOL], src, AX.XY,
                                  ALU.max).then_inc(pool_done, 1)
            dve.wait_ge(pool_done, 18)
            for t in range(9):
                w = pars[0:C, P_DW + t:P_DW + t + 1]
                for b in range(2):
                    o = grid(qkc[:, b * HP:(b + 1) * HP])
                    i = tap(0, t, b * POOL // 2, POOL // 2)
                    if t == 0:
                        ins = dve.tensor_scalar(o, i, w, pars[0:C, P_BDW:P_BDW + 1], ALU.mult, ALU.add)
                    else:
                        dve.wait_ge(qtap_done, 2 * (t - 1) + b + 1)
                        ins = dve.scalar_tensor_tensor(o, i, w, o, ALU.mult, ALU.add)
                    ins.then_inc(qtap_done if t < 8 else qconv_done, 1)
            dve.wait_ge(ssq_done, 2)
            link(dve.tensor_scalar(n2[:, :], ssq[:, :], 1e-24, None, ALU.max))
            link(rsqrt(rnorm[:, :], n2[:, :], n2h[:, :], n2t[:, :], n2u[:, :]))
            dve.tensor_tensor(rqt[:, :], rnorm[:, 0:1], pars[0:C, P_TEMP:P_TEMP + 1], ALU.mult).then_inc(rnorm_done, 1)
            dve.wait_ge(rnorm_done, 1)
            dve.wait_ge(rk_spread, 1)
            link(dve.tensor_tensor(rk_blk[:, :], bank(1, cols=C), cst[0:C, K_BLK:K_BLK + C], ALU.mult))
            dve.wait_ge(score_done, 1)
            link(dve.scalar_tensor_tensor(sc_blk[:, :], bank(0, cols=C), rqt[:, 0:1], rk_blk[:, :], ALU.mult, ALU.mult))
            link(dve.tensor_reduce(sc[:, :], sc_blk[:, :].rearrange("p (h d) -> p d h", d=DH), AX.X, ALU.add))
            dve.tensor_reduce(nmax[:, :], sc[:, :], AX.X, ALU.max, negate=True).then_inc(nmax_done, 1)
            other = sc[:, :].unsqueeze(1).broadcast_to([C, DH, DH])
            own = sc[:, :].unsqueeze(2).broadcast_to([C, DH, DH])
            sq3 = lambda t: t[:, :].rearrange("p (i j) -> p i j", j=DH)
            dve.tensor_tensor(sq3(above), other, own, ALU.is_gt)
            link(dve.tensor_tensor(sq3(equal), other, own, ALU.is_equal))
            link(dve.tensor_tensor(equal[:, :], equal[:, :], cst[0:C, K_TRI:K_TRI + DH * DH], ALU.mult))
            link(dve.tensor_tensor(above[:, :], above[:, :], equal[:, :], ALU.add))
            link(dve.tensor_reduce(rank[:, :], sq3(above), AX.X, ALU.add))
            dve.wait_ge(exp_done, 1)
            for i, k in enumerate(KEEP):
                ins = dve.scalar_tensor_tensor(kept[:, i * DH:(i + 1) * DH], rank[:, :], float(k), ex[:, :],
                                               ALU.is_lt, ALU.mult, accum_out=ksum[:, i:i + 1])
            link(ins)
            link(dve.reciprocal(coef[:, :], ksum[:, :]))
            link(dve.tensor_tensor(coef[:, :], coef[:, :], pars[0:C, P_A:P_A + 4], ALU.mult))
            by_k = lambda t: t[:, :].rearrange("p (k d) -> p k d", d=DH)
            link(dve.tensor_tensor(by_k(scaled), by_k(kept), coef[:, :].unsqueeze(2).broadcast_to([C, 4, DH]),
                                   ALU.mult))
            link(dve.tensor_reduce(att[:, :], scaled[:, :].rearrange("p (k d) -> p d k", d=DH), AX.X, ALU.add))
            dve.tensor_tensor(att_blk[:, :].rearrange("p (h d) -> p h d", d=DH),
                              att[:, :].unsqueeze(1).broadcast_to([C, HEADS, DH]),
                              cst[0:C, K_BLK:K_BLK + C].rearrange("p (h d) -> p h d", d=DH),
                              ALU.mult).then_inc(att_ready, 1)
            dve.wait_ge(attT_done, 1)
            dve.tensor_copy(attT[:, :], bank(4, cols=C)).then_inc(attT_copied, 1)
            dve.wait_ge(x_in, 16)
            dve.wait_ge(proj_ready, 1)
            for y in range(2):
                xv, pv = x2_views(0, y)
                dve.tensor_tensor(xv, xv, pv, ALU.add).then_inc(x2_ready[0], 1)

            def x2_arrives(k):
                if k % TPC == 0:
                    dve.wait_ge(x2T_done, k // TPC + 1)

            ln_vector(1, 1e-5, lambda k: bank(2 + k // TPC, 128, C, at=k % TPC * C), x2_arrives)
            g3 = lambda t: t[:, :].rearrange("p (t e) -> p t e", e=E)
            per_e = lambda t: t[:, :].unsqueeze(2).broadcast_to([128, NT, E])
            g8v = g8[:, :].rearrange("p (t k e) -> p t k e", k=2, e=E)

            def score_steps():
                dve.wait_ge(gscore_copied, 1)
                link(dve.tensor_tensor(g3(gs), g8v[:, :, 0], g8v[:, :, 1], ALU.add))
                link(dve.tensor_reduce(gm[:, :], g3(gs), AX.X, ALU.max))
                dve.tensor_tensor(g3(gs), g3(gs), per_e(gm), ALU.subtract).then_inc(gsub_done, 1)

            def gate_steps():
                dve.wait_ge(gexp_done, 1)
                link(dve.tensor_reduce(gm[:, :], g3(ge), AX.X, ALU.add))
                link(dve.reciprocal(gm[:, :], gm[:, :]))
                link(dve.tensor_tensor(g3(gs), g3(ge), per_e(gm), ALU.mult))
                g4 = lambda t: t[:, :].rearrange("p (t i j) -> p t i j", i=E, j=E)
                gother = g3(gs).unsqueeze(2).broadcast_to([128, NT, E, E])
                gown = g3(gs).unsqueeze(3).broadcast_to([128, NT, E, E])
                link(dve.tensor_tensor(g4(gcmp), gother, gown, ALU.is_gt))
                for i in range(1, E):
                    ins = dve.tensor_tensor(g4(gcmp)[:, :, i, 0:i], gother[:, :, i, 0:i], gown[:, :, i, 0:i],
                                            ALU.is_ge)
                link(ins)
                link(dve.tensor_reduce(grank[:, :], g4(gcmp), AX.X, ALU.add))
                link(dve.scalar_tensor_tensor(gate[:, :], grank[:, :], 2.0, gs[:, :], ALU.is_lt, ALU.mult))
                link(dve.tensor_reduce(gm[:, :], g3(gate), AX.X, ALU.add))
                link(dve.tensor_scalar(gm[:, :], gm[:, :], 1e-9, None, ALU.add))
                link(dve.reciprocal(gm[:, :], gm[:, :]))
                link(dve.tensor_tensor(g3(gate), g3(gate), per_e(gm), ALU.mult))
                part = gparts[:, :].rearrange("p (t k e) -> p t k e", k=3, e=E)
                link(dve.tensor_copy(part[:, :, 0], g3(gate)))
                link(dve.tensor_tensor(g3(gs), g3(gate), part[:, :, 0], ALU.subtract))
                link(dve.tensor_copy(part[:, :, 1], g3(gs)))
                dve.tensor_tensor(part[:, :, 2], g3(gs), part[:, :, 1], ALU.subtract).then_inc(gparts_done, 1)

            def outputs(c, q, first=False):
                for e in finished(q, first):
                    dve.wait_ge(l2_done, c * NH + (e + 1) * HT)
                    dve.wait_ge(gb_copied, c * E + e + 1)
                    if not (first and e < 2):
                        dve.wait_ge(acc_done, c * E + e - 1)
                    dve.scalar_tensor_tensor(cols(yg, e % 2), bank(4 + e % 2, cols=CH),
                                             pars[0:C, P_B2 + e:P_B2 + e + 1], cols(gb, e % 2),
                                             ALU.add, ALU.mult).then_inc(y_gated, 1)

            def chunk(c, first=False):
                for p in range(NPAIR):
                    n = c * NPAIR + p
                    dve.wait_ge(gelu_done, n + 1)
                    if not (first and p < HB):
                        dve.wait_ge(l2_done, 2 * (n - HB + 1))
                    h = cols(hf, p % 2, 2 * CH)
                    hi, lo = cols(h_hi, p % HB, 2 * CH), cols(h_lo, p % HB, 2 * CH)
                    dve.tensor_copy(hi, h).then_inc(h_split, 1)
                    dve.wait_ge(h_split, 2 * n + 1)
                    dve.tensor_tensor(lo, h, hi.bitcast(F32), ALU.subtract).then_inc(h_split, 1)
                    if first and p == 2:
                        score_steps()
                    if first and p == 3:
                        gate_steps()
                    if p >= LAG:
                        outputs(c, p - LAG, first)
                    elif not first:
                        outputs(c - 1, p - LAG + NPAIR)

            chunk(0, True)
            with dve.Fori(1, NCH) as c:
                chunk(c)
            for q in range(NPAIR - LAG, NPAIR):
                outputs(NCH - 1, q)

        @block.tensor
        def _(pe):
            def idle(n, b):
                for _ in range(n):
                    pe.matmul(bank(b, 128), idle_b[:, 0:128], idle_b[:, :], start=True, stop=True)

            def turn_back(i, c):
                if c >= 2:
                    pe.wait_ge(ln[i]["hi"], c - 1)
                which = "by_scalar" if c in BY_SCALAR else "by_vector"
                before = sum((d in BY_SCALAR) == (c in BY_SCALAR) for d in range(c)) * TPC
                if i == 1 and c == HALF:
                    pe.wait_ge(ln[i][which], before + TPC)
                for t in range(TPC):
                    k = c * TPC + t
                    pe.wait_ge(ln[i][which], before + t + 1)
                    ins = pe.transpose(bank(turn_bank(i, c), cols=128, at=t * 128), xnT[:, k * C:(k + 1) * C], ident)
                ins.then_inc(ln[i]["turned"], 1)

            def three(o, w_hi, w_lo, m_hi, m_lo, start=True, stop=True):
                pe.matmul(o, w_hi, m_hi, start=start, stop=False)
                pe.matmul(o, w_lo, m_hi, start=False, stop=False)
                return pe.matmul(o, w_hi, m_lo, start=False, stop=stop)

            pe.wait_ge(idle_set, 1)
            idle(IDLE[0], 3)
            pe.wait_ge(cst_in, 16)
            for n, (g, c) in enumerate(QKV_ORDER):
                if n == 0:
                    for d in range(HALF):
                        turn_back(0, d)
                        idle(IDLE[1], 3)
                    pe.wait_ge(par_split, 2)
                    pe.wait_ge(lastrow_set, 2)
                if n == TURN_AT:
                    for d in range(HALF, NCH):
                        turn_back(0, d)
                if g == 2:
                    pe.wait_ge(ln[0]["lo"], c + 1)
                if n >= 6:
                    pe.wait_ge(pool_done, n - 5)
                w = slice(P_QKV + g * C, P_QKV + (g + 1) * C)
                three(bank(QKV_BANKS[n % 6], cols=CH), par_hi[:, w], par_lo[:, w], cols(xn_hi, c),
                      cols(xn_lo, c)).then_inc(qkv_done, 1)
            pe.wait_ge(pool_done, 16)
            pe.wait_ge(diag_set, 18)
            pe.wait_ge(kp_split, 1)
            for b in range(2):
                for t in range(9):
                    d = slice(t * C, (t + 1) * C)
                    pe.matmul(bank(2 + b, cols=HP), diag_hi[:, d], tap_of(t, kp_hi, b), start=(t == 0), stop=False)
                    pe.matmul(bank(2 + b, cols=HP), diag_lo[:, d], tap_of(t, kp_hi, b), start=False, stop=False)
            pe.wait_ge(kp_split, 2)
            for b in range(2):
                for t in range(9):
                    ins = pe.matmul(bank(2 + b, cols=HP), diag_hi[:, t * C:(t + 1) * C], tap_of(t, kp_lo, b),
                                    start=False, stop=(t == 8))
                ins.then_inc(kconv_done, 1)

            def turn(g, b):
                for t in range(TB // 2):
                    at = g * PIX + b * HP + t * C
                    ins = pe.transpose(bank(4 + 2 * g + b, cols=C, at=t * C), qkc[:, at:at + C], ident[0:C, 0:C])
                ins.then_inc(qkT_done, 1)

            pe.wait_ge(pool_done, 18)
            for b in range(2):
                pe.wait_ge(k_ready, b + 1)
                turn(1, b)
            idle(IDLE[2], 1)
            for b in range(2):
                pe.wait_ge(qconv_done, b + 1)
                turn(0, b)
            idle(IDLE[3], 1)
            pe.wait_ge(qkT_copied, 4)
            for j in range(TB):
                ins = pe.matmul(bank(0, cols=C), qkT[:, j * C:(j + 1) * C], qkT[:, PIX + j * C:PIX + (j + 1) * C],
                                start=(j == 0), stop=(j == TB - 1))
            ins.then_inc(score_done, 1)
            idle(IDLE[7], 5)
            pe.wait_ge(rnorm_done, 1)
            pe.matmul(bank(1, cols=C), rnorm[:, 1:2].broadcast_to([C, C]), ident[0:C, 0:C],
                      start=True, stop=True).then_inc(rk_spread, 1)
            idle(IDLE[4], 5)
            pe.wait_ge(att_ready, 1)
            pe.transpose(bank(4, cols=C), att_blk[:, :], ident[0:C, 0:C]).then_inc(attT_done, 1)
            pe.wait_ge(attT_copied, 1)
            pe.wait_ge(v_ready, 8)
            for b in range(2):
                pe.matmul(bank(6 + b, cols=HP), attT[:, :], vc[:, b * HP:(b + 1) * HP],
                          start=True, stop=True).then_inc(av_done, 1)
            for b in range(2):
                pe.wait_ge(gelu_o, b + 1)
                pe.matmul(bank(b, cols=HP), pars[0:C, P_PROJ:P_PROJ + C], go[:, b * HP:(b + 1) * HP],
                          start=True, stop=True).then_inc(proj_done, 1)
            idle(IDLE[5], 2)
            for c in range(NCH):
                pe.wait_ge(x2_ready[c // HALF], 2)
                for t in range(TPC):
                    k = c * TPC + t
                    ins = pe.transpose(bank(2 + c, 128, C, at=t * C), xs[:, k * 128:(k + 1) * 128], ident[0:C, 0:C])
                ins.then_inc(x2T_done, 1)
            idle(IDLE[6], 0)
            for c in range(HALF):
                turn_back(1, c)

            def gate_scores():
                pe.wait_ge(ln[1]["lo"], NCH)
                pe.wait_ge(gate_split, 2)
                for k in range(NT):
                    w = slice(k * 128, (k + 1) * 128)
                    pe.matmul(bank(7, 128, 2 * E, at=k * 2 * E), xn_hi[:, w], gate_r[:, :], start=True, stop=False,
                              skip_group_check=True)
                    ins = pe.matmul(bank(7, 128, E, at=k * 2 * E), xn_lo[:, w], gate_r[:, 0:E], start=False,
                                    stop=True, skip_group_check=True)
                ins.then_inc(gscore_done, 1)

            def turn_gates():
                pe.wait_ge(gparts_done, 1)
                pe.wait_ge(sel_set, 2)
                for b in range(3):
                    if b == 2:
                        pe.wait_ge(gT_copied, 1)
                    dst = psum[0:3 * E, (6 + b % 2) * BANK:(6 + b % 2) * BANK + 384].bitcast(BF16)
                    for t in range(6):
                        k = b * 6 + t
                        ins = pe.transpose(dst[:, t * 128:(t + 1) * 128],
                                           gparts[:, k * 3 * E:(k + 1) * 3 * E], ident_b[:, :])
                    ins.then_inc(gT_done, 1)

            pe.wait_ge(ln[1]["hi"], HALF)
            pe.wait_ge(ln[1]["lo"], 1)
            pe.wait_ge(w_split, 4)

            def first_product(c, p):
                for j in (2 * p, 2 * p + 1):
                    w = slice(j * 128, (j + 1) * 128)
                    ins = three(bank(2 * (p % 2) + j % 2, 128, CH), w1_hi[:, w], w1_lo[:, w], cols(xn_hi, c),
                                cols(xn_lo, c))
                ins.then_inc(l1_done, 1)

            def second_product(c, q, first=False):
                for e in finished(q, first):
                    if not (first and e < 2):
                        pe.wait_ge(gb_copied, c * E + e - 1)
                    pe.matmul(bank(6 + e % 2, cols=CH), sel_b[:, e * C:(e + 1) * C], cols(gateT, c),
                              start=True, stop=True).then_inc(gb_done, 1)
                pe.wait_ge(h_split, 2 * (c * NPAIR + q + 1))
                for j in (2 * q, 2 * q + 1):
                    e, t = divmod(j, HT)
                    if t == 0 and not (first and e < 2):
                        pe.wait_ge(y_gated, c * E + e - 1)
                    o = bank(4 + e % 2, cols=CH)
                    w = slice(j * C, (j + 1) * C)
                    at = (q % HB) * 2 * CH + (j % 2) * CH
                    ins = three(o, w2_hi[:, w], w2_lo[:, w], h_hi[:, at:at + CH], h_lo[:, at:at + CH],
                                start=(t == 0), stop=(t == HT - 1))
                    ins.then_inc(l2_done, 1)

            def chunk(c, first=False):
                for p in range(NPAIR):
                    if not (first and p < 2):
                        pe.wait_ge(gelu_done, c * NPAIR + p - 1)
                    first_product(c, p)
                    if first and p == 1:
                        for d in range(HALF, NCH):
                            turn_back(1, d)
                        pe.wait_ge(ln[1]["hi"], NCH)
                    if p >= LAG:
                        second_product(c, p - LAG, first)
                    elif not first:
                        second_product(c - 1, p - LAG + NPAIR)
                    if first and p == 2:
                        gate_scores()
                    if first and p == 4:
                        turn_gates()
                        pe.wait_ge(gT_copied, 3)

            chunk(0, True)
            with pe.Fori(1, NCH) as c:
                chunk(c)
            for q in range(NPAIR - LAG, NPAIR):
                second_product(NCH - 1, q)


def _constants():
    import numpy as np
    k = np.zeros((128, K_END), np.float32)
    k[:, K_ID:K_ID + 128] = np.eye(128)
    k[:C, K_BLK:K_BLK + C] = np.kron(np.eye(HEADS), np.ones((DH, DH)))
    k[:, K_TRI:K_TRI + DH * DH] = np.tril(np.ones((DH, DH)), -1).reshape(-1)
    k[:, K_TRIE:K_TRIE + E * E] = np.tril(np.ones((E, E)), -1).reshape(-1)
    return k


def kernel(x, L0_conv_w_qkv, L0_conv_b_qkv, L0_conv_w_dw, L0_conv_b_dw, L0_conv_w_proj, L0_conv_b_proj,
           L0_conv_temperature, L0_conv_a1, L0_conv_a2, L0_conv_a3, L0_conv_a4,
           L0_ffn_gate_w, L0_ffn_gate_b, L0_ffn_w1, L0_ffn_b1, L0_ffn_w2, L0_ffn_b2):
    import numpy as np
    import concourse.bacc as bacc
    from concourse import mybir as mb
    from concourse.bass_utils import run_bass_kernel_spmd as run

    f = lambda a: np.ascontiguousarray(np.asarray(a))
    par = np.zeros((C + 1, P_END), np.float32)
    par[:C, P_QKV:P_QKV + 3 * C] = f(L0_conv_w_qkv).T
    par[C, P_QKV:P_QKV + 3 * C] = f(L0_conv_b_qkv)
    par[:C, P_PROJ:P_PROJ + C] = f(L0_conv_w_proj).T
    par[:C, P_GATE:P_GATE + E] = f(L0_ffn_gate_w)
    par[C, P_GATE:P_GATE + E] = f(L0_ffn_gate_b)
    par[:C, P_DW:P_DW + 27] = f(L0_conv_w_dw).reshape(3, C, 9).transpose(1, 0, 2).reshape(C, 27)
    par[:C, P_BDW:P_BDW + 3] = f(L0_conv_b_dw).reshape(3, C).T
    par[:C, P_BPROJ] = f(L0_conv_b_proj)
    par[:C, P_TEMP] = np.repeat(f(L0_conv_temperature).reshape(-1), DH)
    for i, a in enumerate((L0_conv_a1, L0_conv_a2, L0_conv_a3, L0_conv_a4)):
        par[:C, P_A + i] = f(a)[0]
    par[:C, P_B2:P_B2 + E] = f(L0_ffn_b2).T
    arrays = {
        "x": f(x).reshape(C, TOK),
        "xt": f(f(x).reshape(C, NT, 128).transpose(2, 1, 0)).reshape(128, NT * C),
        "par": par,
        "b1": f(L0_ffn_b1).reshape(1, E * HID),
        "w1": f(L0_ffn_w1),
        "w2": f(L0_ffn_w2),
        "consts": _constants(),
        "sel": np.tile(np.repeat(np.eye(E, dtype=np.float32), C, axis=1), (3, 1)),
    }
    nc = bacc.Bacc("TRN2", target_bir_lowering=False, num_devices=1)
    args = [nc.dram_tensor(n, a.shape, mb.dt.float32, kind="ExternalInput").ap() for n, a in arrays.items()]
    out = nc.dram_tensor("out", (C, TOK), mb.dt.float32, kind="ExternalOutput").ap()
    build(nc, *args, out)
    r = run(nc, [arrays], core_ids=[0])
    return r.results[0]["out"].reshape(1, C, IMG, IMG)
```

```python
import concourse.bass as bass
from concourse import mybir
from contextlib import ExitStack

F32 = mybir.dt.float32
F32R = mybir.dt.float32r
BF16 = mybir.dt.bfloat16
I32 = mybir.dt.int32
ALU = mybir.AluOpType
ACT = mybir.ActivationFunctionType
AX = mybir.AxisListType

C = 96
IMG = 48
TOK = IMG * IMG
POOL = IMG // 2
PIX = POOL * POOL
PAD = POOL + 2
HEADS = 8
DH = C // HEADS
KEEP = (DH // 2, DH * 2 // 3, DH * 3 // 4, DH * 4 // 5)
E = 4
HID = 4 * C
HT = HID // 128
NH = E * HT
CH = 384
NCH = TOK // CH
TPC = CH // 128
NT = TOK // 128
HALF = NCH // 2
NPAIR = NH // 2
LAG = 2
IDLE = {"start": 29, "first turned back": 8, "before q": 0, "before scores": 2,
        "softmax": 7, "projected": 2, "normalised": 4, "scored": 2}
IDLE_TURN = ((0, 3, 3, 0, 0, 0), (0, 2, 2, 2, 0, 5))
IDLE_SCORES = (0, 0, 1, 0, 0, 0)
IDLE_FIRST = (0, 0, 0, 0, 2, 0)
LN_GROUPS = ((0, 3, 6), (0, 2, 4, 6))
BY_SCALAR = (1, 5)
LOW_AFTER = 3
SECOND_HALF_TURNS = {1: (3,), 2: (4,), 4: (5,)}
TURNS_IN_FIRST = ((1, 2), (3,), (4, 5), (), (), ())
QKV_BANKS = (0, 1, 2, 3, 6, 7)
HIGH_BY_SCALAR = ((1,), (0, 2), (0, 2, 4))
SPLIT_EARLY = 1
KEPT = 6
TURN_GATES_AT = 2
SECOND_CHUNK = {3: ((0, 0), (0, 1)), 4: ((0, 2), (0, 3)), 5: ((1, 0), (1, 1))}
RSQRT_STEPS = 8
HB = 3
BANK = 512
TB = PIX // C
HP = PIX // 2

P_QKV = 0
P_PROJ = P_QKV + 3 * C
P_GATE = P_PROJ + C
P_DW = P_GATE + E
P_SPLIT = P_DW + 27
P_BDW = P_SPLIT
P_BPROJ = P_BDW + 3
P_TEMP = P_BPROJ + 1
P_A = P_TEMP + 1
P_B2 = P_A + 4
P_END = P_B2 + E

K_ID = 0
K_BLK = K_ID + 128
K_TRI = K_BLK + C
K_END = K_TRI + DH * DH


QKV_ORDER = [(g, c) for half in range(2) for g in (2, 1, 0) for c in range(half * HALF, (half + 1) * HALF)]


def finished(q):
    return tuple(e for e in range(E) if (HT * e + HT - 1) // 2 == q)


def gated_now(c, p):
    if is_chunk(c, 0):
        return ()
    if is_chunk(c, 1):
        return SECOND_CHUNK.get(p, ())
    if p < LAG:
        return tuple((c - 1, e) for e in finished(p - LAG + NPAIR))
    return tuple((c, e) for e in finished(p - LAG))


def is_kept(c, e):
    return isinstance(c, int) and c * E + e < KEPT


def high_by_scalar(c, p):
    if is_chunk(c, 0):
        return p in HIGH_BY_SCALAR[0]
    return p in HIGH_BY_SCALAR[1 if is_chunk(c, 1) else 2]


def hi_count(c, p):
    each = [NPAIR - len(done) for done in HIGH_BY_SCALAR]
    now = p + 1 - sum(high_by_scalar(c, q) for q in range(p + 1))
    if is_chunk(c, 0):
        return now
    if is_chunk(c, 1):
        return each[0] + now
    return each[0] + each[1] + (c - 2) * each[2] + now


def is_chunk(c, n):
    return isinstance(c, int) and c == n


def build(nc, x, xt, par, b1, w1, w2, const, sel, out):
    ctx = ExitStack()
    with ctx:
        def sb(name, shape, dt=F32):
            return ctx.enter_context(nc.sbuf_tensor(name, shape, dt))

        def sem(name):
            return ctx.enter_context(nc.semaphore(name))

        psum = ctx.enter_context(nc.psum_tensor("psum", [128, 8 * BANK], F32))

        def bank(b, rows=C, cols=BANK, at=0):
            return psum[0:rows, b * BANK + at:b * BANK + at + cols]

        xs = sb("xs", [C, TOK])
        pars = sb("pars", [C + 1, P_END])
        cst = sb("cst", [128, K_END])
        ident = cst[:, K_ID:K_ID + 128]
        ident_b = sb("ident_b", [128, 128], BF16)
        sel_b = sb("sel_b", [128, E * C], BF16)
        sels = sb("sels", [3 * E, E * C])
        gate_r = sb("gate_r", [C + 1, 2 * E], F32R)
        w1s = sb("w1s", [C + 1, E * HID])
        w1_hi = sb("w1_hi", [C + 1, E * HID], F32R)
        w1_lo = sb("w1_lo", [C + 1, E * HID], F32R)
        w2s = sb("w2s", [128, NH * C])
        w2_hi = sb("w2_hi", [128, NH * C], F32R)
        w2_lo = sb("w2_lo", [128, NH * C], F32R)
        xT = sb("xT", [128, NT * C])
        xnT = sb("xnT", [128, NT * C])
        stats = sb("stats", [128, NT * 6])
        mv = sb("mv", [128, NT * 2])
        xn = sb("xn", [C, TOK])
        xn_hi = sb("xn_hi", [C + 1, TOK], F32R)
        xn_lo = sb("xn_lo", [C + 1, TOK], F32R)
        var = sb("var", [128, NT])
        seed = sb("seed", [128, NT])
        nhalf = sb("nhalf", [128, NT])
        newton = sb("newton", [128, NT])
        newton2 = sb("newton2", [128, NT])
        nmr = sb("nmr", [128, NT])
        pooled = sb("pooled", [C, 3 * PAD * PAD])
        qkc = sb("qkc", [C, 2 * PIX])
        qkT = sb("qkT", [C, 2 * PIX])
        vc = sb("vc", [C, PIX])
        par_hi = sb("par_hi", [C + 1, P_SPLIT], F32R)
        par_lo = sb("par_lo", [C + 1, P_SPLIT], F32R)
        diag_hi = sb("diag_hi", [C, 9 * C], F32R)
        diag_lo = sb("diag_lo", [C, 9 * C], F32R)
        kp_hi = sb("kp_hi", [C, PAD * PAD], F32R)
        kp_lo = sb("kp_lo", [C, PAD * PAD], F32R)
        idle_b = sb("idle_b", [128, BANK], BF16)
        sqj = sb("sqj", [C, PIX])
        ssq = sb("ssq", [C, 2])
        n2 = sb("n2", [C, 2])
        n2h = sb("n2h", [C, 2])
        n2t = sb("n2t", [C, 2])
        n2u = sb("n2u", [C, 2])
        rnorm = sb("rnorm", [C, 2])
        rqt = sb("rqt", [C, 1])
        sq_blk = sb("sq_blk", [C, C])
        sc_blk = sb("sc_blk", [C, C])
        sc = sb("sc", [C, DH])
        nmax = sb("nmax", [C, 1])
        ex = sb("ex", [C, DH])
        above = sb("above", [C, DH * DH])
        equal = sb("equal", [C, DH * DH])
        rank = sb("rank", [C, DH])
        kept = sb("kept", [C, 4 * DH])
        ksum = sb("ksum", [C, 4])
        coef = sb("coef", [C, 4])
        scaled = sb("scaled", [C, 4 * DH])
        att = sb("att", [C, DH])
        att_blk = sb("att_blk", [C, C])
        attT = sb("attT", [C, C])
        go = sb("go", [C, PIX])
        pr = sb("pr", [C, HP])
        g8 = sb("g8", [128, NT * 2 * E])
        vprod = sb("vprod", [C, 2 * PIX])
        gs = sb("gs", [128, NT * E])
        gm = sb("gm", [128, NT])
        ge = sb("ge", [128, NT * E])
        ginv = sb("ginv", [128, NT])
        gcmp = sb("gcmp", [128, NT * E * E])
        grank = sb("grank", [128, NT * E])
        gate = sb("gate", [128, NT * E])
        gparts = sb("gparts", [128, NT * 3 * E], BF16)
        gateT = sb("gateT", [128, TOK], BF16)
        gb = sb("gb", [C, E * CH])
        hf = sb("hf", [128, 2 * 2 * CH])
        h_hi = sb("h_hi", [128, HB * 2 * CH], F32R)
        h_lo = sb("h_lo", [128, HB * 2 * CH], F32R)
        y0 = sb("y0", [C, KEPT * CH])
        yg = sb("yg", [C, E * CH])

        x_in = sem("x_in")
        xt_in = [sem(f"xt_in{i}") for i in range(2)]
        sel_in = sem("sel_in")
        par_in, cst_in, w1_in, w2_in = sem("par_in"), sem("cst_in"), sem("w1_in"), sem("w2_in")
        ones_set = sem("ones_set")
        idle_set = sem("idle_set")
        par_split = sem("par_split")
        kp_split = sem("kp_split")
        lastrow_set = sem("lastrow_set")
        ident_set = sem("ident_set")
        diag_set = sem("diag_set")
        sel_set = sem("sel_set")
        w_split = sem("w_split")
        dve_chain = sem("dve_chain")
        ln = [{n: sem(f"ln{i}_{n}") for n in
               ("stats", "rstd", "by_vector", "by_scalar", "turned", "hi", "lo")} for i in range(2)]
        x2T_done = sem("x2T_done")
        gate_split = sem("gate_split")
        qkv_done, pool_done = sem("qkv_done"), sem("pool_done")
        kconv_done, k_ready = sem("kconv_done"), sem("k_ready")
        qtap_done, qconv_done = sem("qtap_done"), sem("qconv_done")
        vprod_done, v_ready = sem("vprod_done"), sem("v_ready")
        ssq_done, rnorm_done = sem("ssq_done"), sem("rnorm_done")
        qkT_done, qkT_copied = sem("qkT_done"), sem("qkT_copied")
        rk_spread, score_done = sem("rk_spread"), sem("score_done")
        nmax_done, exp_done = sem("nmax_done"), sem("exp_done")
        att_ready, attT_done, attT_copied = sem("att_ready"), sem("attT_done"), sem("attT_copied")
        av_done, gelu_o, proj_done, proj_ready = sem("av_done"), sem("gelu_o"), sem("proj_done"), sem("proj_ready")
        x2_ready = [sem("x2_ready_vector"), sem("x2_ready_gpsimd")]
        gscore_done, gscore_copied, gsub_done, gexp_done, gparts_done = (
            sem("gscore_done"), sem("gscore_copied"), sem("gsub_done"), sem("gexp_done"), sem("gparts_done"))
        gT_done, gT_copied = sem("gT_done"), sem("gT_copied")
        l1_done, gelu_done, h_split, l2_done = sem("l1_done"), sem("gelu_done"), sem("h_split"), sem("l2_done")
        hi_copied = sem("hi_copied")
        gb_done, gb_copied, y_gated, acc_done = sem("gb_done"), sem("gb_copied"), sem("y_gated"), sem("acc_done")
        y0_done = sem("y0_done")
        gchain = sem("gate_chain")
        gcompared, ginv_done = sem("gcompared"), sem("ginv_done")
        out_done = sem("out_done")

        block = ctx.enter_context(nc.Block())

        def padded(g):
            return pooled[:, g * PAD * PAD:(g + 1) * PAD * PAD].rearrange("p (a b) -> p a b", b=PAD)

        def tap(g, t, r0=0, rows=POOL):
            dy, dx = divmod(t, 3)
            return padded(g)[:, r0 + dy:r0 + dy + rows, dx:dx + POOL]

        def by_tile(t):
            return t[:, :].rearrange("p (t e) -> p t e", e=E)

        def per_expert(t):
            return t[:, :].unsqueeze(2).broadcast_to([128, NT, E])

        def grid(ap):
            return ap.rearrange("p (a b) -> p a b", b=POOL)

        def turn_bank(i, c):
            if i == 0:
                return 4 + c % 2
            return 2 + c if c else 0

        def v_buffer(t):
            ap, at = (vprod, t - 7) if t >= 7 else (xnT, t - 4) if t >= 4 else (xT, t - 1)
            return ap[0:C, at * PIX:(at + 1) * PIX]

        def tap_of(t, ap, b):
            dy, dx = divmod(t, 3)
            r = b * POOL // 2 + dy
            return ap[:, :].rearrange("p (a b) -> p a b", b=PAD)[:, r:r + POOL // 2, dx:dx + POOL]

        def x2_views(ap, c0, c1, y):
            rows = CH // IMG // 2
            first = c0 % HALF * rows * POOL
            xv = xs[:, c0 * CH:c1 * CH].rearrange("p (a y b x) -> p y a b x", y=2, b=POOL, x=2)
            pv = grid(ap[:, first:first + (c1 - c0) * rows * POOL])
            return xv[:, y], pv.unsqueeze(3).broadcast_to([C, (c1 - c0) * rows, POOL, 2])

        def cols(ap, c, n=CH):
            return ap[:, bass.ds(c * n, n)]

        @block.sync
        def _(sp):
            hw = NT // 2 * C
            sp.dma_start(xT[:, 0:hw], xt[:, 0:hw]).then_inc(xt_in[0], 16)
            sp.dma_start(pars[:, :], par).then_inc(par_in, 16)
            sp.dma_start(w1s[0:C, :].rearrange("p (e h) -> p e h", e=E),
                         w1.rearrange("e d h -> d e h")).then_inc(w1_in, 16)
            sp.dma_start(w1s[C:C + 1, :], b1).then_inc(w1_in, 16)
            sp.dma_start(w2s[:, :].rearrange("p (j d) -> p j d", d=C),
                         w2.rearrange("e (t p) d -> p (e t) d", p=128)).then_inc(w2_in, 16)
            with sp.Fori(0, NCH) as c:
                sp.wait_ge(acc_done, c * E + E)
                sp.dma_start(out[:, bass.ds(c * CH, CH)], cols(xs, c)).then_inc(out_done, 16)
            sp.wait_ge(out_done, 16 * NCH)

        @block.gpsimd
        def _(pool):
            def low(dst, src, hi, done):
                return pool.tensor_tensor(dst, src, hi.bitcast(F32), ALU.subtract).then_inc(done, 1)

            def split_gates():
                pool.wait_ge(ginv_done, 1)
                pool.tensor_tensor(by_tile(gate), by_tile(gate), per_expert(ginv), ALU.mult).then_inc(gchain, 1)
                part = gparts[:, :].rearrange("p (t k e) -> p t k e", k=3, e=E)
                pool.wait_ge(gchain, 1)
                pool.tensor_copy(part[:, :, 0], by_tile(gate)).then_inc(gchain, 1)
                pool.wait_ge(gchain, 2)
                pool.tensor_tensor(by_tile(gs), by_tile(gate), part[:, :, 0], ALU.subtract).then_inc(gchain, 1)
                pool.wait_ge(gchain, 3)
                pool.tensor_copy(part[:, :, 1], by_tile(gs)).then_inc(gchain, 1)
                pool.wait_ge(gchain, 4)
                pool.tensor_tensor(part[:, :, 2], by_tile(gs), part[:, :, 1], ALU.subtract).then_inc(gparts_done, 1)

            pool.memset(pooled[:, :], 0.0).then_inc(ones_set, 1)
            pool.wait_ge(ones_set, 1)
            pool.memset(xn_hi[C:C + 1, :].bitcast(F32), 1.0).then_inc(lastrow_set, 1)
            pool.memset(xn_lo[C:C + 1, :].bitcast(F32), 0.0).then_inc(lastrow_set, 1)
            pool.wait_ge(lastrow_set, 2)
            pool.wait_ge(par_in, 16)
            pool.wait_ge(par_split, 1)
            low(par_lo[:, :], pars[:, 0:P_SPLIT], par_hi[:, :], par_split)
            pool.wait_ge(par_split, 2)
            pool.wait_ge(cst_in, 16)

            def low_diagonal(t):
                w = P_DW + 9 + t
                pool.tensor_scalar(diag_lo[:, t * C:(t + 1) * C], ident[0:C, 0:C],
                                   par_lo[0:C, w:w + 1].bitcast(F32), None, ALU.mult).then_inc(diag_set, 1)

            for t in range(5):
                low_diagonal(t)
            for c in range(NCH):
                pool.wait_ge(ln[0]["hi"], c + 1)
                low(cols(xn_lo, c)[0:C], cols(xn, c), cols(xn_hi, c)[0:C], ln[0]["lo"])
            for t in range(5, 9):
                low_diagonal(t)
            pool.wait_ge(kp_split, 1)
            low(kp_lo[:, :], pooled[:, PAD * PAD:2 * PAD * PAD], kp_hi[:, :], kp_split)
            for t in range(1, 9):
                pool.wait_ge(vprod_done, t + 1)
                if t >= 2:
                    pool.wait_ge(v_ready, t - 1)
                pool.tensor_tensor(vc[:, :], vc[:, :], v_buffer(t), ALU.add).then_inc(v_ready, 1)
            pool.wait_ge(w_split, 2)
            low(w1_lo[:, :], w1s[:, :], w1_hi[:, :], w_split)
            pool.wait_ge(w_split, 3)
            low(w2_lo[:, :], w2s[:, :], w2_hi[:, :], w_split)
            pool.wait_ge(w_split, 4)
            pool.wait_ge(gate_split, 1)
            low(gate_r[:, E:2 * E], pars[:, P_GATE:P_GATE + E], gate_r[:, 0:E], gate_split)
            pool.wait_ge(gate_split, 2)
            pool.wait_ge(x_in, 16)
            pool.wait_ge(proj_ready, 1)
            for y in range(2):
                xv, pv = x2_views(pr[:, :], HALF, NCH, y)
                pool.tensor_tensor(xv, xv, pv, ALU.add).then_inc(x2_ready[1], 1)
            pool.wait_ge(x2_ready[1], 2)
            pool.memset(gateT[:, :].bitcast(F32), 0.0).then_inc(ones_set, 1)
            pool.memset(sel_b[:, :].bitcast(F32), 0.0).then_inc(sel_set, 1)
            pool.wait_ge(sel_set, 1)
            pool.wait_ge(ones_set, 2)
            pool.wait_ge(sel_in, 16)
            pool.tensor_copy(sel_b[0:3 * E, :], sels[:, :]).then_inc(sel_set, 1)
            pool.wait_ge(sel_set, 2)
            pool.wait_ge(ln[1]["lo"], 1)
            for c in range(1, NCH):
                pool.wait_ge(ln[1]["hi"], c + 1)
                low(cols(xn_lo, c)[0:C], cols(xn, c), cols(xn_hi, c)[0:C], ln[1]["lo"])
            pool.wait_ge(ln[1]["lo"], NCH)
            split_gates()
            for c in range(NCH):
                for e in range(E if c < NCH - 1 else E - 1):
                    pool.wait_ge(y_gated, c * E + e + 1)
                    if e:
                        pool.wait_ge(acc_done, c * E + e)
                    pool.tensor_tensor(cols(xs, c), cols(xs, c), cols(yg, e), ALU.add).then_inc(acc_done, 1)

        @block.scalar
        def _(act):
            hw = NT // 2 * C
            act.dma_start(cst[:, :], const).then_inc(cst_in, 16)
            act.dma_start(xT[:, hw:], xt[:, hw:]).then_inc(xt_in[1], 16)
            act.dma_start(sels[:, :], sel).then_inc(sel_in, 16)
            act.dma_start(xs[:, :], x).then_inc(x_in, 16)
            act.wait_ge(cst_in, 16)
            act.activation(ident_b[:, :], ident, ACT.Copy).then_inc(ident_set, 1)
            act.wait_ge(par_in, 16)
            act.activation(par_hi[:, :], pars[:, 0:P_SPLIT], ACT.Copy).then_inc(par_split, 1)
            act.activation(gate_r[:, 0:E], pars[:, P_GATE:P_GATE + E], ACT.Copy).then_inc(gate_split, 1)

            for t in range(9):
                w = P_DW + 9 + t
                act.activation(diag_hi[:, t * C:(t + 1) * C], ident[0:C, 0:C], ACT.Copy,
                               scale=pars[0:C, w:w + 1]).then_inc(diag_set, 1)

            def normalise(i, c, src):
                act.wait_ge(ln[i]["rstd"], sum(c >= d for d in LN_GROUPS[i]))
                for k in range(c * TPC, (c + 1) * TPC):
                    act.activation(xnT[:, k * C:(k + 1) * C], src(k), ACT.Identity, scale=seed[:, k:k + 1],
                                   bias=nmr[:, k:k + 1]).then_inc(ln[i]["by_scalar"], 1)

            def take(i, c):
                act.wait_ge(ln[i]["turned"], c + 1)
                act.activation(cols(xn_hi, c)[0:C], bank(turn_bank(i, c), cols=CH), ACT.Copy)
                act.activation(cols(xn, c), bank(turn_bank(i, c), cols=CH), ACT.Copy).then_inc(ln[i]["hi"], 1)

            for half in range(2):
                normalise(0, BY_SCALAR[half], lambda k: xT[:, k * C:(k + 1) * C])
                for c in range(half * HALF, (half + 1) * HALF):
                    take(0, c)
            act.wait_ge(w1_in, 32)
            act.activation(w1_hi[:, :], w1s[:, :], ACT.Copy).then_inc(w_split, 1)
            act.wait_ge(w2_in, 16)
            act.activation(w2_hi[:, :], w2s[:, :], ACT.Copy).then_inc(w_split, 1)

            def v_product(t):
                w = pars[0:C, P_DW + 18 + t:P_DW + 19 + t]
                if t == 0:
                    act.activation(grid(vc[:, :]), tap(2, t), ACT.Identity, scale=w,
                                   bias=pars[0:C, P_BDW + 2:P_BDW + 3]).then_inc(vprod_done, 1)
                else:
                    act.activation(grid(v_buffer(t)), tap(2, t), ACT.Copy, scale=w).then_inc(vprod_done, 1)

            act.wait_ge(pool_done, 12)
            v_product(0)
            v_product(1)
            act.wait_ge(pool_done, 15)
            act.activation(kp_hi[:, :], pooled[:, PAD * PAD:2 * PAD * PAD], ACT.Copy).then_inc(kp_split, 1)
            for t in range(2, 9):
                v_product(t)
            for b in range(2):
                act.wait_ge(kconv_done, b + 1)
                act.activation(qkc[:, PIX + b * HP:PIX + (b + 1) * HP], bank(2 + b, cols=HP), ACT.Identity,
                               bias=pars[0:C, P_BDW + 1:P_BDW + 2]).then_inc(k_ready, 1)
            act.wait_ge(k_ready, 2)
            act.activation(sqj[:, :], qkc[:, PIX:], ACT.Square, accum_out=ssq[:, 1:2]).then_inc(ssq_done, 1)
            for g in (1, 0):
                for b in range(2):
                    act.wait_ge(qkT_done, 2 * (1 - g) + b + 1)
                    act.activation(qkT[:, g * PIX + b * HP:g * PIX + (b + 1) * HP],
                                   bank(4 + 2 * g + b, cols=HP), ACT.Copy).then_inc(qkT_copied, 1)
            act.wait_ge(nmax_done, 1)
            act.activation(ex[:, :], sc[:, :], ACT.Exp, bias=nmax[:, 0:1]).then_inc(exp_done, 1)
            for b in range(2):
                act.wait_ge(av_done, b + 1)
                act.activation(go[:, b * HP:(b + 1) * HP], bank(6 + b, cols=HP), ACT.Gelu).then_inc(gelu_o, 1)
            act.wait_ge(proj_done, 2)
            act.activation(pr[:, :], bank(1, cols=HP), ACT.Identity,
                           bias=pars[0:C, P_BPROJ:P_BPROJ + 1]).then_inc(proj_ready, 1)
            x2_tile = lambda k: bank(2 + k // TPC, 128, C, at=k % TPC * C)
            act.wait_ge(ln[1]["turned"], 1)
            act.activation(cols(xn_hi, 0)[0:C], bank(turn_bank(1, 0), cols=CH), ACT.Copy).then_inc(ln[1]["hi"], 1)
            normalise(1, BY_SCALAR[0], x2_tile)

            def gelu(c, p):
                act.wait_ge(l1_done, c * NPAIR + p + 1)
                if not (is_chunk(c, 0) and p < 2):
                    act.wait_ge(h_split, c * NPAIR + p - 1)
                src = psum[:, (p % 2) * 2 * BANK:(p % 2 + 1) * 2 * BANK].rearrange(
                    "p (j n) -> p j n", n=BANK)[:, :, 0:CH]
                if high_by_scalar(c, p):
                    if not (is_chunk(c, 0) and p < HB):
                        act.wait_ge(l2_done, 2 * (c * NPAIR + p - HB + 1))
                    act.activation(cols(h_hi, p % HB, 2 * CH).rearrange("p (j n) -> p j n", n=CH), src, ACT.Gelu)
                act.activation(cols(hf, p % 2, 2 * CH).rearrange("p (j n) -> p j n", n=CH), src,
                               ACT.Gelu).then_inc(gelu_done, 1)

            def gates(c, e):
                act.wait_ge(gb_done, c * E + e + 1)
                if not is_chunk(c, 0):
                    act.wait_ge(y_gated, (c - 1) * E + e + 1)
                act.activation(cols(gb, e), bank(6 + e % 2, cols=CH), ACT.Copy).then_inc(gb_copied, 1)

            def take_gates(b):
                act.wait_ge(gT_done, b + 1)
                act.activation(gateT[0:3 * E, b * 768:(b + 1) * 768],
                               psum[0:3 * E, (6 + b % 2) * BANK:(6 + b % 2) * BANK + 384].bitcast(BF16),
                               ACT.Copy).then_inc(gT_copied, 1)

            def keep_outputs(c, q):
                for e in finished(q):
                    if c * E + e < KEPT:
                        act.wait_ge(l2_done, c * NH + (e + 1) * HT)
                        act.activation(cols(y0, c * E + e), bank(4 + e % 2, cols=CH), ACT.Identity,
                                       bias=pars[0:C, P_B2 + e:P_B2 + e + 1]).then_inc(y0_done, 1)

            def chunk(c):
                for p in range(NPAIR):
                    gelu(c, p)
                    if is_chunk(c, 0):
                        if p == 1:
                            normalise(1, BY_SCALAR[1], x2_tile)
                        for d in TURNS_IN_FIRST[p]:
                            take(1, d)
                        if p == 4:
                            act.wait_ge(gscore_done, NCH)
                            act.activation(g8[:, :], bank(7, 128, NT * 2 * E), ACT.Copy).then_inc(gscore_copied, 1)
                        if p >= LAG:
                            keep_outputs(c, p - LAG)
                        if p == 4:
                            act.wait_ge(gsub_done, 1)
                            act.activation(ge[:, :], gs[:, :], ACT.Exp).then_inc(gexp_done, 1)
                    if is_chunk(c, 1):
                        if p == TURN_GATES_AT + 1:
                            take_gates(2)
                        if p < LAG:
                            keep_outputs(0, p - LAG + NPAIR)
                        else:
                            keep_outputs(1, p - LAG)
                        if p == TURN_GATES_AT:
                            act.wait_ge(ones_set, 2)
                            take_gates(0)
                            take_gates(1)
                    for d, e in gated_now(c, p):
                        gates(d, e)

            chunk(0)
            chunk(1)
            with act.Fori(2, NCH) as c:
                chunk(c)
            for q in range(NPAIR - LAG, NPAIR):
                for e in finished(q):
                    gates(NCH - 1, e)

        @block.vector
        def _(dve):
            chain = [0]

            def link(ins, beside=None, step=0):
                chain[0] += 1
                ins.then_inc(dve_chain, 1)
                if beside:
                    beside(step)
                dve.wait_ge(dve_chain, chain[0])

            def rsqrt(y, v, nh, t, u, beside=None):
                dve.tensor_scalar(nh, v, -0.5, None, ALU.mult)
                link(dve.tensor_scalar(y.bitcast(I32), v.bitcast(I32), -0.5, 1597463007.0, ALU.mult, ALU.add),
                     beside, 1)
                link(dve.tensor_tensor(t, y, y, ALU.mult), beside, 2)
                link(dve.tensor_tensor(t, t, nh, ALU.mult), beside, 3)
                dve.scalar_tensor_tensor(y, t, 1.5, y, ALU.add, ALU.mult)
                link(dve.scalar_tensor_tensor(u, t, 1.5, t, ALU.add, ALU.mult), beside, 4)
                link(dve.scalar_tensor_tensor(t, t, 1.5, u, ALU.add, ALU.mult), beside, 5)
                link(dve.scalar_tensor_tensor(y, t, 1.5, y, ALU.add, ALU.mult), beside, 6)
                link(dve.tensor_tensor(t, y, y, ALU.mult), beside, 7)
                link(dve.tensor_tensor(t, t, nh, ALU.mult), beside, 8)
                return dve.scalar_tensor_tensor(y, t, 1.5, y, ALU.add, ALU.mult)

            def low_of_first(c=0):
                dve.wait_ge(ln[1]["hi"], c + 1)
                dve.tensor_tensor(cols(xn_lo, c)[0:C], bank(turn_bank(1, c), cols=CH),
                                  cols(xn_hi, c)[0:C].bitcast(F32), ALU.subtract).then_inc(ln[1]["lo"], 1)

            def split(c, p):
                n = c * NPAIR + p
                dve.wait_ge(gelu_done, n + 1)
                if not (is_chunk(c, 0) and p < HB):
                    dve.wait_ge(l2_done, 2 * (n - HB + 1))
                h = cols(hf, p % 2, 2 * CH)
                hi, lo = cols(h_hi, p % HB, 2 * CH), cols(h_lo, p % HB, 2 * CH)
                if not high_by_scalar(c, p):
                    dve.tensor_copy(hi, h).then_inc(hi_copied, 1)
                    dve.wait_ge(hi_copied, hi_count(c, p))
                dve.tensor_tensor(lo, h, hi.bitcast(F32), ALU.subtract).then_inc(h_split, 1)

            def ln_vector(i, eps, src, ready):
                done = ln[i]["stats"]
                moments = mv[:, :].rearrange("p (t k) -> p t k", k=2)
                groups = [list(range(c * TPC, d * TPC)) for c, d in zip(LN_GROUPS[i], LN_GROUPS[i][1:])]
                own = [[k for k in tiles if k // TPC not in BY_SCALAR] for tiles in groups]

                def statistics(k):
                    ready(k)
                    dve.bn_stats(stats[:, k * 6:(k + 1) * 6], src(k)).then_inc(done, 1)

                def normalise(k):
                    dve.tensor_scalar(xnT[:, k * C:(k + 1) * C], src(k), mv[:, 2 * k:2 * k + 1],
                                      seed[:, k:k + 1], ALU.subtract, ALU.mult).then_inc(ln[i]["by_vector"], 1)

                for k in groups[0]:
                    statistics(k)
                for n, tiles in enumerate(groups):
                    z = slice(tiles[0], tiles[-1] + 1)
                    for k in tiles:
                        dve.wait_ge(done, k + 1)
                        ins = dve.bn_aggr(mv[:, 2 * k:2 * k + 2], stats[:, k * 6:(k + 1) * 6])
                    before = own[n - 1] if n > i else []
                    after = groups[n + 1] if n + 1 < len(groups) else []

                    def beside(step):
                        if i == 1 and n == 1 and step == LOW_AFTER:
                            low_of_first()
                        if step < len(before):
                            normalise(before[step])
                        elif step - len(before) < len(after):
                            statistics(after[step - len(before)])

                    link(ins, beside, 0)
                    link(dve.tensor_scalar(var[:, z], moments[:, z, 1], eps, None, ALU.add))
                    link(rsqrt(seed[:, z], var[:, z], nhalf[:, z], newton[:, z], newton2[:, z], beside))
                    dve.scalar_tensor_tensor(nmr[:, z], moments[:, z, 0], -1.0, seed[:, z], ALU.mult,
                                             ALU.mult).then_inc(ln[i]["rstd"], 1)
                    if i == 1 and n == 0:
                        for k in own[0]:
                            normalise(k)
                    for step in range(RSQRT_STEPS + 1, len(before) + len(after)):
                        beside(step)
                if i == 1:
                    for p in range(SPLIT_EARLY):
                        split(0, p)
                for k in own[-1]:
                    normalise(k)

            def x_arrives(k):
                if k % (NT // 2) == 0:
                    dve.wait_ge(xt_in[k // (NT // 2)], 16)

            dve.memset(idle_b[:, :].bitcast(F32), 0.0).then_inc(idle_set, 1)
            ln_vector(0, 1e-6, lambda k: xT[:, k * C:(k + 1) * C], x_arrives)
            dve.wait_ge(ones_set, 1)
            for n, (g, c) in enumerate(QKV_ORDER):
                dve.wait_ge(qkv_done, n + 1)
                src = bank(QKV_BANKS[n % 6], cols=CH).rearrange("p (a y b x) -> p a b y x", y=2, b=POOL, x=2)
                dve.tensor_reduce(padded(g)[:, 1 + 4 * c:5 + 4 * c, 1:1 + POOL], src, AX.XY,
                                  ALU.max).then_inc(pool_done, 1)
            dve.wait_ge(pool_done, 18)
            for t in range(9):
                w = pars[0:C, P_DW + t:P_DW + t + 1]
                for b in range(2):
                    o = grid(qkc[:, b * HP:(b + 1) * HP])
                    i = tap(0, t, b * POOL // 2, POOL // 2)
                    if t == 0:
                        ins = dve.tensor_scalar(o, i, w, pars[0:C, P_BDW:P_BDW + 1], ALU.mult, ALU.add)
                    else:
                        dve.wait_ge(qtap_done, 2 * (t - 1) + b + 1)
                        ins = dve.scalar_tensor_tensor(o, i, w, o, ALU.mult, ALU.add)
                    ins.then_inc(qtap_done if t < 8 else qconv_done, 1)
            dve.wait_ge(qconv_done, 2)
            dve.wait_ge(ssq_done, 1)
            q = qkc[:, 0:PIX]
            link(dve.scalar_tensor_tensor(sqj[:, :], q, 1.0, q, ALU.mult, ALU.mult, accum_out=ssq[:, 0:1]))
            link(dve.tensor_scalar(n2[:, :], ssq[:, :], 1e-24, None, ALU.max))
            rsqrt(rnorm[:, :], n2[:, :], n2h[:, :], n2t[:, :], n2u[:, :]).then_inc(rnorm_done, 1)
            dve.wait_ge(rnorm_done, 1)
            link(dve.tensor_tensor(rqt[:, :], rnorm[:, 0:1], pars[0:C, P_TEMP:P_TEMP + 1], ALU.mult))
            dve.wait_ge(score_done, 1)
            link(dve.scalar_tensor_tensor(sq_blk[:, :], bank(0, cols=C), rqt[:, 0:1], cst[0:C, K_BLK:K_BLK + C],
                                          ALU.mult, ALU.mult))
            dve.wait_ge(rk_spread, 1)
            link(dve.tensor_tensor(sc_blk[:, :], sq_blk[:, :], bank(1, cols=C), ALU.mult))
            link(dve.tensor_reduce(sc[:, :], sc_blk[:, :].rearrange("p (h d) -> p d h", d=DH), AX.X, ALU.add))
            dve.tensor_reduce(nmax[:, :], sc[:, :], AX.X, ALU.max, negate=True).then_inc(nmax_done, 1)
            other = sc[:, :].unsqueeze(1).broadcast_to([C, DH, DH])
            own = sc[:, :].unsqueeze(2).broadcast_to([C, DH, DH])
            sq3 = lambda t: t[:, :].rearrange("p (i j) -> p i j", j=DH)
            dve.tensor_tensor(sq3(above), other, own, ALU.is_gt)
            link(dve.tensor_tensor(sq3(equal), other, own, ALU.is_equal))
            link(dve.tensor_tensor(equal[:, :], equal[:, :], cst[0:C, K_TRI:K_TRI + DH * DH], ALU.mult))
            link(dve.tensor_tensor(above[:, :], above[:, :], equal[:, :], ALU.add))
            link(dve.tensor_reduce(rank[:, :], sq3(above), AX.X, ALU.add))
            dve.wait_ge(exp_done, 1)
            for i, k in enumerate(KEEP):
                ins = dve.scalar_tensor_tensor(kept[:, i * DH:(i + 1) * DH], rank[:, :], float(k), ex[:, :],
                                               ALU.is_lt, ALU.mult, accum_out=ksum[:, i:i + 1])
            link(ins)
            link(dve.reciprocal(coef[:, :], ksum[:, :]))
            link(dve.tensor_tensor(coef[:, :], coef[:, :], pars[0:C, P_A:P_A + 4], ALU.mult))
            by_k = lambda t: t[:, :].rearrange("p (k d) -> p k d", d=DH)
            link(dve.tensor_tensor(by_k(scaled), by_k(kept), coef[:, :].unsqueeze(2).broadcast_to([C, 4, DH]),
                                   ALU.mult))
            link(dve.tensor_reduce(att[:, :], scaled[:, :].rearrange("p (k d) -> p d k", d=DH), AX.X, ALU.add))
            dve.tensor_tensor(att_blk[:, :].rearrange("p (h d) -> p h d", d=DH),
                              att[:, :].unsqueeze(1).broadcast_to([C, HEADS, DH]),
                              cst[0:C, K_BLK:K_BLK + C].rearrange("p (h d) -> p h d", d=DH),
                              ALU.mult).then_inc(att_ready, 1)
            dve.wait_ge(attT_done, 1)
            dve.tensor_copy(attT[:, :], bank(4, cols=C)).then_inc(attT_copied, 1)
            dve.wait_ge(x_in, 16)
            dve.wait_ge(proj_done, 1)
            for c0, c1 in ((0, 1), (1, HALF)):
                for y in range(2):
                    xv, pv = x2_views(bank(0, cols=HP), c0, c1, y)
                    dve.scalar_tensor_tensor(xv, pv, pars[0:C, P_BPROJ:P_BPROJ + 1], xv, ALU.add,
                                             ALU.add).then_inc(x2_ready[0], 1)

            def x2_arrives(k):
                if k % TPC == 0:
                    dve.wait_ge(x2T_done, k // TPC + 1)

            ln_vector(1, 1e-5, lambda k: bank(2 + k // TPC, 128, C, at=k % TPC * C), x2_arrives)
            def scores_less_maximum():
                dve.wait_ge(gscore_copied, 1)
                g8v = g8[:, :].rearrange("p (t k e) -> p t k e", k=2, e=E)
                link(dve.tensor_tensor(by_tile(gs), g8v[:, :, 0], g8v[:, :, 1], ALU.add))
                link(dve.tensor_reduce(gm[:, :], by_tile(gs), AX.X, ALU.max))
                dve.tensor_tensor(by_tile(gs), by_tile(gs), per_expert(gm), ALU.subtract).then_inc(gsub_done, 1)

            def compare_experts():
                dve.wait_ge(gexp_done, 1)
                link(dve.tensor_reduce(gm[:, :], by_tile(ge), AX.X, ALU.add))
                link(dve.reciprocal(gm[:, :], gm[:, :]))
                link(dve.tensor_tensor(by_tile(gs), by_tile(ge), per_expert(gm), ALU.mult))
                g4 = gcmp[:, :].rearrange("p (t i j) -> p t i j", i=E, j=E)
                other = by_tile(gs).unsqueeze(2).broadcast_to([128, NT, E, E])
                own = by_tile(gs).unsqueeze(3).broadcast_to([128, NT, E, E])
                link(dve.tensor_tensor(g4, other, own, ALU.is_gt))
                for i in range(1, E):
                    dve.tensor_tensor(g4[:, :, i, 0:i], other[:, :, i, 0:i], own[:, :, i, 0:i],
                                      ALU.is_ge).then_inc(gcompared, 1)

            def sum_chosen():
                dve.wait_ge(gcompared, E - 1)
                g4 = gcmp[:, :].rearrange("p (t i j) -> p t i j", i=E, j=E)
                link(dve.tensor_reduce(grank[:, :], g4, AX.X, ALU.add))
                link(dve.scalar_tensor_tensor(gate[:, :], grank[:, :], 2.0, gs[:, :], ALU.is_lt, ALU.mult))
                link(dve.tensor_reduce(gm[:, :], by_tile(gate), AX.X, ALU.add))
                link(dve.tensor_scalar(gm[:, :], gm[:, :], 1e-9, None, ALU.add))
                dve.reciprocal(ginv[:, :], gm[:, :]).then_inc(ginv_done, 1)

            def output(c, e):
                dve.wait_ge(gb_copied, c * E + e + 1)
                if not is_chunk(c, 0):
                    dve.wait_ge(acc_done, (c - 1) * E + e + 1)
                if is_kept(c, e):
                    dve.wait_ge(y0_done, c * E + e + 1)
                    dve.tensor_tensor(cols(yg, e), cols(y0, c * E + e), cols(gb, e), ALU.mult).then_inc(y_gated, 1)
                else:
                    dve.wait_ge(l2_done, c * NH + (e + 1) * HT)
                    dve.scalar_tensor_tensor(cols(yg, e), bank(4 + e % 2, cols=CH),
                                             pars[0:C, P_B2 + e:P_B2 + e + 1], cols(gb, e),
                                             ALU.add, ALU.mult).then_inc(y_gated, 1)

            def chunk(c):
                for p in range(NPAIR):
                    if is_chunk(c, 0) and p == 4:
                        scores_less_maximum()
                    if is_chunk(c, 0) and p == 5:
                        compare_experts()
                    if not (is_chunk(c, 0) and p < SPLIT_EARLY):
                        split(c, p)
                    if is_chunk(c, 0) and p == 5:
                        sum_chosen()
                    for d, e in gated_now(c, p):
                        output(d, e)

            chunk(0)
            chunk(1)
            with dve.Fori(2, NCH) as c:
                chunk(c)
            for q in range(NPAIR - LAG, NPAIR):
                for e in finished(q):
                    output(NCH - 1, e)
            dve.wait_ge(y_gated, NCH * E)
            dve.wait_ge(acc_done, NCH * E - 1)
            dve.tensor_tensor(cols(xs, NCH - 1), cols(xs, NCH - 1), cols(yg, E - 1), ALU.add).then_inc(acc_done, 1)

        @block.tensor
        def _(pe):
            def idle(n, b):
                for _ in range(n):
                    pe.matmul(bank(b, 128), idle_b[:, 0:128], idle_b[:, :], start=True, stop=True)

            def turn_back(i, c):
                if i == 0 and c >= 2:
                    pe.wait_ge(ln[i]["hi"], c - 1)
                which = "by_scalar" if c in BY_SCALAR else "by_vector"
                before = sum((d in BY_SCALAR) == (c in BY_SCALAR) for d in range(c)) * TPC
                if i == 1 and c:
                    pe.wait_ge(ln[i][which], before + TPC)
                idle(IDLE_TURN[i][c], turn_bank(i, c))
                for t in range(TPC):
                    k = c * TPC + t
                    pe.wait_ge(ln[i][which], before + t + 1)
                    ins = pe.transpose(bank(turn_bank(i, c), cols=128, at=t * 128), xnT[:, k * C:(k + 1) * C], ident)
                ins.then_inc(ln[i]["turned"], 1)

            def three(o, w_hi, w_lo, m_hi, m_lo, start=True, stop=True):
                pe.matmul(o, w_hi, m_hi, start=start, stop=False)
                pe.matmul(o, w_lo, m_hi, start=False, stop=False)
                return pe.matmul(o, w_hi, m_lo, start=False, stop=stop)

            pe.wait_ge(idle_set, 1)
            idle(IDLE["start"], 3)
            pe.wait_ge(cst_in, 16)
            for n, (g, c) in enumerate(QKV_ORDER):
                if n == 0:
                    for d in range(HALF):
                        turn_back(0, d)
                    pe.wait_ge(par_split, 2)
                    pe.wait_ge(lastrow_set, 2)
                for d in SECOND_HALF_TURNS.get(n, ()):
                    turn_back(0, d)
                if g == 2:
                    pe.wait_ge(ln[0]["lo"], c + 1)
                if n >= 6:
                    pe.wait_ge(pool_done, n - 5)
                w = slice(P_QKV + g * C, P_QKV + (g + 1) * C)
                three(bank(QKV_BANKS[n % 6], cols=CH), par_hi[:, w], par_lo[:, w], cols(xn_hi, c),
                      cols(xn_lo, c)).then_inc(qkv_done, 1)
            pe.wait_ge(pool_done, 16)
            pe.wait_ge(diag_set, 18)
            pe.wait_ge(kp_split, 1)
            for b in range(2):
                for t in range(9):
                    d = slice(t * C, (t + 1) * C)
                    pe.matmul(bank(2 + b, cols=HP), diag_hi[:, d], tap_of(t, kp_hi, b), start=(t == 0), stop=False)
                    pe.matmul(bank(2 + b, cols=HP), diag_lo[:, d], tap_of(t, kp_hi, b), start=False, stop=False)
            pe.wait_ge(kp_split, 2)
            for b in range(2):
                for t in range(9):
                    ins = pe.matmul(bank(2 + b, cols=HP), diag_hi[:, t * C:(t + 1) * C], tap_of(t, kp_lo, b),
                                    start=False, stop=(t == 8))
                ins.then_inc(kconv_done, 1)

            def turn(g, b):
                for t in range(TB // 2):
                    at = g * PIX + b * HP + t * C
                    ins = pe.transpose(bank(4 + 2 * g + b, cols=C, at=t * C), qkc[:, at:at + C], ident[0:C, 0:C])
                ins.then_inc(qkT_done, 1)

            pe.wait_ge(pool_done, 18)
            for b in range(2):
                pe.wait_ge(k_ready, b + 1)
                turn(1, b)
            idle(IDLE["before q"], 1)
            for b in range(2):
                pe.wait_ge(qconv_done, b + 1)
                turn(0, b)
            idle(IDLE["before scores"], 1)
            pe.wait_ge(qkT_copied, 4)
            for j in range(TB):
                ins = pe.matmul(bank(0, cols=C), qkT[:, j * C:(j + 1) * C], qkT[:, PIX + j * C:PIX + (j + 1) * C],
                                start=(j == 0), stop=(j == TB - 1))
            ins.then_inc(score_done, 1)
            idle(IDLE["scored"], 5)
            pe.wait_ge(rnorm_done, 1)
            pe.matmul(bank(1, cols=C), rnorm[:, 1:2].broadcast_to([C, C]), ident[0:C, 0:C],
                      start=True, stop=True).then_inc(rk_spread, 1)
            idle(IDLE["softmax"], 5)
            pe.wait_ge(att_ready, 1)
            pe.transpose(bank(4, cols=C), att_blk[:, :], ident[0:C, 0:C]).then_inc(attT_done, 1)
            pe.wait_ge(attT_copied, 1)
            pe.wait_ge(v_ready, 8)
            for b in range(2):
                pe.matmul(bank(6 + b, cols=HP), attT[:, :], vc[:, b * HP:(b + 1) * HP],
                          start=True, stop=True).then_inc(av_done, 1)
            for b in range(2):
                pe.wait_ge(gelu_o, b + 1)
                pe.matmul(bank(b, cols=HP), pars[0:C, P_PROJ:P_PROJ + C], go[:, b * HP:(b + 1) * HP],
                          start=True, stop=True).then_inc(proj_done, 1)
            idle(IDLE["projected"], 2)
            for c in range(NCH):
                pe.wait_ge(x2_ready[c // HALF], 4 if 0 < c < HALF else 2)
                for t in range(TPC):
                    k = c * TPC + t
                    ins = pe.transpose(bank(2 + c, 128, C, at=t * C), xs[:, k * 128:(k + 1) * 128], ident[0:C, 0:C])
                ins.then_inc(x2T_done, 1)
            idle(IDLE["normalised"], 0)
            turn_back(1, 0)

            def gate_scores(d):
                pe.wait_ge(ln[1]["lo"], d + 1)
                for k in range(d * TPC, (d + 1) * TPC):
                    w = slice(k * 128, (k + 1) * 128)
                    pe.matmul(bank(7, 128, 2 * E, at=k * 2 * E), xn_hi[:, w], gate_r[:, :], start=True, stop=False,
                              skip_group_check=True)
                    ins = pe.matmul(bank(7, 128, E, at=k * 2 * E), xn_lo[:, w], gate_r[:, 0:E], start=False,
                                    stop=True, skip_group_check=True)
                ins.then_inc(gscore_done, 1)
                idle(IDLE_SCORES[d], 6)

            def turn_gates(b):
                if b == 0:
                    pe.wait_ge(gparts_done, 1)
                    pe.wait_ge(sel_set, 2)
                if b == 2:
                    pe.wait_ge(gT_copied, 1)
                dst = psum[0:3 * E, (6 + b % 2) * BANK:(6 + b % 2) * BANK + 384].bitcast(BF16)
                for t in range(6):
                    k = b * 6 + t
                    ins = pe.transpose(dst[:, t * 128:(t + 1) * 128],
                                       gparts[:, k * 3 * E:(k + 1) * 3 * E], ident_b[:, :])
                ins.then_inc(gT_done, 1)

            idle(IDLE["first turned back"], 1)
            pe.wait_ge(ln[1]["hi"], 1)
            pe.wait_ge(ln[1]["lo"], 1)
            pe.wait_ge(w_split, 4)

            def first_product(c, p):
                for j in (2 * p, 2 * p + 1):
                    w = slice(j * 128, (j + 1) * 128)
                    ins = three(bank(2 * (p % 2) + j % 2, 128, CH), w1_hi[:, w], w1_lo[:, w], cols(xn_hi, c),
                                cols(xn_lo, c))
                ins.then_inc(l1_done, 1)

            def spread(c, e):
                if not (is_chunk(c, 0) and e < 2):
                    pe.wait_ge(gb_copied, c * E + e - 1)
                elif e == 0:
                    pe.wait_ge(gT_copied, 3)
                pe.matmul(bank(6 + e % 2, cols=CH), sel_b[:, e * C:(e + 1) * C], cols(gateT, c),
                          start=True, stop=True).then_inc(gb_done, 1)

            def output_bank_free(c, e):
                if is_chunk(c, 0) and e < 2:
                    return
                if is_kept(c, e - 2):
                    pe.wait_ge(y0_done, c * E + e - 1)
                else:
                    pe.wait_ge(y_gated, c * E + e - 1)

            def second_product(c, q):
                pe.wait_ge(h_split, c * NPAIR + q + 1)
                for j in (2 * q, 2 * q + 1):
                    e, t = divmod(j, HT)
                    if t == 0:
                        output_bank_free(c, e)
                    o = bank(4 + e % 2, cols=CH)
                    w = slice(j * C, (j + 1) * C)
                    at = (q % HB) * 2 * CH + (j % 2) * CH
                    ins = three(o, w2_hi[:, w], w2_lo[:, w], h_hi[:, at:at + CH], h_lo[:, at:at + CH],
                                start=(t == 0), stop=(t == HT - 1))
                    ins.then_inc(l2_done, 1)

            def chunk(c):
                for p in range(NPAIR):
                    if not (is_chunk(c, 0) and p < 2):
                        pe.wait_ge(gelu_done, c * NPAIR + p - 1)
                    if is_chunk(c, 0) and p == 1:
                        pe.wait_ge(ln[1]["hi"], 2)
                    if is_chunk(c, 0):
                        idle(IDLE_FIRST[p], 2 * (p % 2))
                    first_product(c, p)
                    if is_chunk(c, 0):
                        if p < LAG:
                            for d in TURNS_IN_FIRST[p]:
                                turn_back(1, d)
                        if p == LAG:
                            pe.wait_ge(ln[1]["hi"], 3)
                        if p == LAG + 1:
                            pe.wait_ge(ln[1]["hi"], NCH)
                            pe.wait_ge(gate_split, 2)
                            gate_scores(0)
                            gate_scores(1)
                        if p == LAG + 2:
                            gate_scores(4)
                            gate_scores(5)
                    if is_chunk(c, 1) and p == TURN_GATES_AT + 1:
                        turn_gates(2)
                    if p >= LAG:
                        second_product(c, p - LAG)
                    elif not is_chunk(c, 0):
                        second_product(c - 1, p - LAG + NPAIR)
                    if is_chunk(c, 0) and p == LAG:
                        for d in TURNS_IN_FIRST[p]:
                            turn_back(1, d)
                    if is_chunk(c, 0) and p == LAG + 1:
                        gate_scores(2)
                        gate_scores(3)
                    if is_chunk(c, 1) and p == TURN_GATES_AT:
                        turn_gates(0)
                        turn_gates(1)
                    for d, e in gated_now(c, p):
                        spread(d, e)

            chunk(0)
            chunk(1)
            with pe.Fori(2, NCH) as c:
                chunk(c)
            for q in range(NPAIR - LAG, NPAIR):
                for e in finished(q):
                    spread(NCH - 1, e)
                second_product(NCH - 1, q)


def _constants():
    import numpy as np
    k = np.zeros((128, K_END), np.float32)
    k[:, K_ID:K_ID + 128] = np.eye(128)
    k[:C, K_BLK:K_BLK + C] = np.kron(np.eye(HEADS), np.ones((DH, DH)))
    k[:, K_TRI:K_TRI + DH * DH] = np.tril(np.ones((DH, DH)), -1).reshape(-1)
    return k


def kernel(x, L0_conv_w_qkv, L0_conv_b_qkv, L0_conv_w_dw, L0_conv_b_dw, L0_conv_w_proj, L0_conv_b_proj,
           L0_conv_temperature, L0_conv_a1, L0_conv_a2, L0_conv_a3, L0_conv_a4,
           L0_ffn_gate_w, L0_ffn_gate_b, L0_ffn_w1, L0_ffn_b1, L0_ffn_w2, L0_ffn_b2):
    import numpy as np
    import concourse.bacc as bacc
    from concourse import mybir as mb
    from concourse.bass_utils import run_bass_kernel_spmd as run

    f = lambda a: np.ascontiguousarray(np.asarray(a))
    par = np.zeros((C + 1, P_END), np.float32)
    par[:C, P_QKV:P_QKV + 3 * C] = f(L0_conv_w_qkv).T
    par[C, P_QKV:P_QKV + 3 * C] = f(L0_conv_b_qkv)
    par[:C, P_PROJ:P_PROJ + C] = f(L0_conv_w_proj).T
    par[:C, P_GATE:P_GATE + E] = f(L0_ffn_gate_w)
    par[C, P_GATE:P_GATE + E] = f(L0_ffn_gate_b)
    par[:C, P_DW:P_DW + 27] = f(L0_conv_w_dw).reshape(3, C, 9).transpose(1, 0, 2).reshape(C, 27)
    par[:C, P_BDW:P_BDW + 3] = f(L0_conv_b_dw).reshape(3, C).T
    par[:C, P_BPROJ] = f(L0_conv_b_proj)
    par[:C, P_TEMP] = np.repeat(f(L0_conv_temperature).reshape(-1), DH)
    for i, a in enumerate((L0_conv_a1, L0_conv_a2, L0_conv_a3, L0_conv_a4)):
        par[:C, P_A + i] = f(a)[0]
    par[:C, P_B2:P_B2 + E] = f(L0_ffn_b2).T
    arrays = {
        "x": f(x).reshape(C, TOK),
        "xt": f(f(x).reshape(C, NT, 128).transpose(2, 1, 0)).reshape(128, NT * C),
        "par": par,
        "b1": f(L0_ffn_b1).reshape(1, E * HID),
        "w1": f(L0_ffn_w1),
        "w2": f(L0_ffn_w2),
        "consts": _constants(),
        "sel": np.tile(np.repeat(np.eye(E, dtype=np.float32), C, axis=1), (3, 1)),
    }
    nc = bacc.Bacc("TRN2", target_bir_lowering=False, num_devices=1)
    args = [nc.dram_tensor(n, a.shape, mb.dt.float32, kind="ExternalInput").ap() for n, a in arrays.items()]
    out = nc.dram_tensor("out", (C, TOK), mb.dt.float32, kind="ExternalOutput").ap()
    build(nc, *args, out)
    r = run(nc, [arrays], core_ids=[0])
    return r.results[0]["out"].reshape(1, C, IMG, IMG)
```
